# Optimizing a Trainium2 kernel written in Bass

```python
import numpy as np
import jax
import jax.numpy as jnp

def _softmax(x, axis=-1):
    return jax.nn.softmax(x, axis=axis)

def _gelu(x):
    return jax.nn.gelu(x, approximate=True)

def _silu(x):
    return jax.nn.silu(x)

def _sigmoid(x):
    return jax.nn.sigmoid(x)

def _layernorm(x, axis=-1, eps=1e-05):
    m = jnp.mean(x, axis=axis, keepdims=True)
    v = jnp.var(x, axis=axis, keepdims=True)
    return (x - m) / jnp.sqrt(v + eps)

def _scatter_add(tgt, idx, src, axis=0):
    return tgt.at[idx].add(src)

def _segment_sum(src, seg, n):
    return jax.ops.segment_sum(src, seg, n)
kernel_name = 'mk_seq_postln_d1_jaxref_r8_5776bb'

def setup_inputs(seed: int=0):
    np.random.seed(seed)
    _w = jnp.asarray

    def _L0_attn_setup():
        import jax, jax.numpy as jnp
        import numpy as np
        EMBED_DIM = 128
        VALUE_DIM = 256
        NUM_HEADS = 8
        KEY_DIM = EMBED_DIM // NUM_HEADS
        HEAD_DIM = VALUE_DIM // NUM_HEADS
        EPS = 1e-05
        B, S = (2, 256)

        def _xavier(k, shape, gain):
            a = gain * np.sqrt(6.0 / (shape[0] + shape[1]))
            return jax.random.uniform(k, shape, jnp.float32, -a, a)

        def _rel_pos(slen):
            lin = jnp.linspace(0.0, 1.0, KEY_DIM // 2)
            angle = jnp.repeat(1.0 / 10000.0 ** lin, 2)
            decay = jnp.log1p(-2.0 ** (-5.0 - jnp.arange(NUM_HEADS, dtype=jnp.float32)))
            idx = jnp.arange(slen, dtype=jnp.float32)
            sin = jnp.sin(idx[:, None] * angle[None, :])
            cos = jnp.cos(idx[:, None] * angle[None, :])
            diff = idx[:, None] - idx[None, :]
            m = jnp.where(diff[None] >= 0, jnp.exp(diff[None] * decay[:, None, None]), 0.0)
            m = m / jnp.sqrt(m.sum(-1, keepdims=True))
            return (sin, cos, m)

        def _rotate_every_two(x):
            x1 = x[..., ::2]
            x2 = x[..., 1::2]
            return jnp.stack((-x2, x1), axis=-1).reshape(x.shape)
        key = jax.random.key(seed)
        ks = jax.random.split(key, 6)
        g = 2.0 ** (-2.5)
        return {'x': jax.random.normal(ks[0], (B, S, EMBED_DIM), jnp.float32), 'wq': _xavier(ks[1], (EMBED_DIM, EMBED_DIM), g), 'wk': _xavier(ks[2], (EMBED_DIM, EMBED_DIM), g), 'wv': _xavier(ks[3], (EMBED_DIM, VALUE_DIM), g), 'wg': _xavier(ks[4], (EMBED_DIM, VALUE_DIM), g), 'wo': _xavier(ks[5], (VALUE_DIM, EMBED_DIM), 1.0)}
    _L0_attn_in = _L0_attn_setup()

    def _L0_ffn_setup():
        import jax, jax.numpy as jnp
        import numpy as np
        E = 8
        H = 128
        F = 128
        K = 2
        B, T = (2, 128)
        key = jax.random.key(seed)
        k1, k2, k3, k4 = jax.random.split(key, 4)
        return {'hidden_states': jax.random.normal(k1, (B, T, H), dtype=jnp.float32), 'router_weight': jax.random.normal(k2, (E, H), dtype=jnp.float32), 'gate_up_proj': jax.random.normal(k3, (E, 2 * F, H), dtype=jnp.float32), 'down_proj': jax.random.normal(k4, (E, H, F), dtype=jnp.float32)}
    _L0_ffn_in = _L0_ffn_setup()
    _d = {'L0_attn_x': _L0_attn_in['x'], 'L0_attn_wq': _L0_attn_in['wq'], 'L0_attn_wk': _L0_attn_in['wk'], 'L0_attn_wv': _L0_attn_in['wv'], 'L0_attn_wg': _L0_attn_in['wg'], 'L0_attn_wo': _L0_attn_in['wo'], 'L0_ffn_router_weight': _L0_ffn_in['router_weight'], 'L0_ffn_gate_up_proj': _L0_ffn_in['gate_up_proj'], 'L0_ffn_down_proj': _L0_ffn_in['down_proj']}
    _x0 = _d['L0_attn_x']
    _d['L0_attn_x'] = jax.random.normal(jax.random.fold_in(jax.random.key(seed), 1), (8, 1024, 128), dtype=_x0.dtype)
    del _x0
    return _d

def reference(L0_attn_x, L0_attn_wq, L0_attn_wk, L0_attn_wv, L0_attn_wg, L0_attn_wo, L0_ffn_router_weight, L0_ffn_gate_up_proj, L0_ffn_down_proj):

    def _L0_attn_ref(x, wq, wk, wv, wg, wo):
        import jax, jax.numpy as jnp
        import numpy as np
        EMBED_DIM = 128
        VALUE_DIM = 256
        NUM_HEADS = 8
        KEY_DIM = EMBED_DIM // NUM_HEADS
        HEAD_DIM = VALUE_DIM // NUM_HEADS
        EPS = 1e-05
        B, S = (2, 256)

        def _xavier(k, shape, gain):
            a = gain * np.sqrt(6.0 / (shape[0] + shape[1]))
            return jax.random.uniform(k, shape, jnp.float32, -a, a)

        def _rel_pos(slen):
            lin = jnp.linspace(0.0, 1.0, KEY_DIM // 2)
            angle = jnp.repeat(1.0 / 10000.0 ** lin, 2)
            decay = jnp.log1p(-2.0 ** (-5.0 - jnp.arange(NUM_HEADS, dtype=jnp.float32)))
            idx = jnp.arange(slen, dtype=jnp.float32)
            sin = jnp.sin(idx[:, None] * angle[None, :])
            cos = jnp.cos(idx[:, None] * angle[None, :])
            diff = idx[:, None] - idx[None, :]
            m = jnp.where(diff[None] >= 0, jnp.exp(diff[None] * decay[:, None, None]), 0.0)
            m = m / jnp.sqrt(m.sum(-1, keepdims=True))
            return (sin, cos, m)

        def _rotate_every_two(x):
            x1 = x[..., ::2]
            x2 = x[..., 1::2]
            return jnp.stack((-x2, x1), axis=-1).reshape(x.shape)
        b, s, _ = x.shape
        sin, cos, mask = _rel_pos(s)
        q = x @ wq
        k = x @ wk * KEY_DIM ** (-0.5)
        v = x @ wv
        g = x @ wg
        q = q.reshape(b, s, NUM_HEADS, KEY_DIM).transpose(0, 2, 1, 3)
        k = k.reshape(b, s, NUM_HEADS, KEY_DIM).transpose(0, 2, 1, 3)
        qr = q * cos + _rotate_every_two(q) * sin
        kr = k * cos + _rotate_every_two(k) * sin
        vr = v.reshape(b, s, NUM_HEADS, HEAD_DIM).transpose(0, 2, 1, 3)
        qk = jnp.einsum('bhik,bhjk->bhij', qr, kr) * mask[None]
        denom = jnp.clip(jnp.abs(jax.lax.stop_gradient(qk).sum(-1, keepdims=True)), 1.0, None)
        qk = qk / denom
        out = jnp.einsum('bhij,bhjd->bihd', qk, vr)
        out = out * jax.lax.rsqrt(jnp.mean(out * out, axis=-1, keepdims=True) + EPS)
        out = out.reshape(b, s, VALUE_DIM)
        out = jax.nn.silu(g) * out
        return out @ wo

    def _L0_ffn_ref(hidden_states, router_weight, gate_up_proj, down_proj):
        import jax, jax.numpy as jnp
        import numpy as np
        E = 8
        H = 128
        F = 128
        K = 2
        B, T = (2, 128)
        b, t, h_dim = hidden_states.shape
        h = hidden_states.reshape(-1, h_dim)
        logits = h @ router_weight.T
        probs = jax.nn.softmax(logits, axis=-1)
        top_v, top_i = jax.lax.top_k(probs, K)
        top_v = top_v / top_v.sum(axis=-1, keepdims=True)
        combine = (jax.nn.one_hot(top_i, E, dtype=top_v.dtype) * top_v[..., None]).sum(axis=1)
        combine = combine.T

        def body(acc, xs):
            gu, dp, w = xs
            gate, up = jnp.split(h @ gu.T, 2, axis=-1)
            out = jax.nn.silu(gate) * up @ dp.T
            return (acc + w[:, None] * out, None)
        acc0 = jnp.zeros_like(h)
        final, _ = jax.lax.scan(body, acc0, (gate_up_proj, down_proj, combine))
        return final.reshape(b, t, h_dim)
    x = L0_attn_x
    x = _layernorm(x + _L0_attn_ref(x, L0_attn_wq, L0_attn_wk, L0_attn_wv, L0_attn_wg, L0_attn_wo), axis=-1)
    x = _layernorm(x + _L0_ffn_ref(x, L0_ffn_router_weight, L0_ffn_gate_up_proj, L0_ffn_down_proj), axis=-1)
    return x

_drawn_inputs = setup_inputs


def setup_inputs(seed=0):
    import zlib

    import numpy as np

    out = dict(_drawn_inputs(seed))
    spreads = {}
    factors = {}
    for name, (base, spread) in spreads.items():
        noise = np.random.default_rng([zlib.crc32(name.encode()), seed]).standard_normal(out[name].shape)
        drawn = base * np.exp(spread * noise) if base else spread * noise
        out[name] = jnp.asarray(drawn.astype(out[name].dtype))
    for name, factor in factors.items():
        out[name] = (out[name] * factor).astype(out[name].dtype)
    return out
```

```python
from contextlib import ExitStack

import numpy as np
import concourse.bass as bass
from concourse import mybir

F32 = mybir.dt.float32
F32R = mybir.dt.float32r
BF16 = mybir.dt.bfloat16
I32 = mybir.dt.int32
ALU = mybir.AluOpType
ACT = mybir.ActivationFunctionType
AX_X = mybir.AxisListType.X
ds = bass.ds

B, S, D = 8, 1024, 128
H, KD, HD = 8, 16, 32
V = H * HD
HA = HD + 1
E, F = 8, 128
P = 128
POS = S // P
PAIRS = POS // 2
NPAIR = B * PAIRS
GROUPS = NPAIR // 2
GT = 4 * P
NCH = B * POS
EPS = 1e-5
RSQRT_MAGIC = float(0x5F3759DF)
NEWTON_LINKS = 2 + 3 * 3

C_ID, C_TRI, C_DECAY = 0, 128, 256
C_GAMMA = C_DECAY + H * HA
C_EVEN, C_ODD = C_GAMMA + 1, C_GAMMA + 2
C_GUARD = C_ODD + 1
C_IDX = C_GUARD + POS * H
C_SEL = C_IDX + E
C_END = C_SEL + E * P


def shape_constants():
    c = np.zeros((P, C_END), np.float32)
    t = np.arange(P)
    decay = np.log1p(-2.0 ** (-5.0 - np.arange(H)))
    c[:, C_ID:C_ID + P] = np.eye(P)
    c[:, C_TRI:C_TRI + P] = t[:, None] <= t[None, :]
    head = t // KD
    block = (head[:, None] == np.arange(H)[None, :]) * np.exp(P * decay)[None, :]
    c[:, C_DECAY:C_GAMMA] = np.repeat(block, HA, axis=1)
    c[:, C_GAMMA] = np.exp(P * decay)[head]
    c[:, C_EVEN] = head % 2 == 0
    c[:, C_ODD] = head % 2 == 1
    i = np.arange(S)
    total = (1 - np.exp((i[:, None] + 1) * decay)) / (1 - np.exp(decay))
    guard = HD * EPS * total * np.exp(-2 * (i % P)[:, None] * decay)
    c[:, C_GUARD:C_IDX] = guard.reshape(POS, P, H).transpose(1, 0, 2).reshape(P, POS * H)
    c[:, C_IDX:C_SEL] = E - np.arange(E)
    sel = np.zeros((P, E, P))
    for e in range(E):
        sel[e, e] = sel[E + e, e] = 1
    c[:, C_SEL:] = sel.reshape(P, E * P)
    at = np.arange(KD // 2, dtype=np.float32) * np.float32(1 / (KD // 2 - 1))
    angle = np.repeat((1 / 10000.0 ** at.astype(np.float64)).astype(np.float32), 2)
    phase = (i.astype(np.float32)[:, None] * angle[None, :]).astype(np.float64)
    sign = np.where(np.arange(KD) % 2 == 0, -1.0, 1.0)
    kscale = KD ** -0.5 * np.exp(-(i % P)[:, None] * decay)
    out = []
    for table in (np.cos(phase), np.sin(phase) * sign):
        q = np.tile(table, (1, H))
        k = (kscale[:, :, None] * table[:, None, :]).reshape(S, H * KD)
        both = np.concatenate([q, k], axis=1).reshape(POS, P, 2 * D)
        out.append(both.transpose(1, 0, 2).reshape(P, POS * 2 * D).astype(np.float32))
    return c, out[0], out[1]


def wait(eng, sem, value):
    if isinstance(value, int) and value <= 0:
        return
    eng.wait_ge(sem, value)


def within(n, end):
    return not isinstance(n, int) or 0 <= n < end


class Chain:

    def __init__(self, eng, sem, base):
        self.eng, self.sem, self.base, self.n = eng, sem, base, 0

    def step(self, ins):
        self.n += 1
        ins.then_inc(self.sem, 1)

    def wait(self):
        wait(self.eng, self.sem, self.base + self.n)

    def __call__(self, ins):
        self.step(ins)
        self.wait()


def newton_rsqrt(v, link, x, y, t, scale):
    link(v.tensor_scalar(t.bitcast(I32), x.bitcast(I32), 1, None, ALU.logical_shift_right))
    link(v.tensor_scalar(y.bitcast(I32), t.bitcast(I32), -1.0, RSQRT_MAGIC, ALU.mult, ALU.add))
    for n in range(3):
        last = scale if n == 2 else 1.0
        link(v.scalar_tensor_tensor(out=t, in0=y, scalar=-0.5, in1=y, op0=ALU.mult, op1=ALU.mult))
        link(v.tensor_tensor(t, t, x, ALU.mult))
        if last == 1.0:
            link(v.scalar_tensor_tensor(out=y, in0=t, scalar=1.5, in1=y, op0=ALU.add, op1=ALU.mult))
        else:
            link(v.tensor_scalar(t, t, 1.5, last, ALU.add, ALU.mult))
    if scale != 1.0:
        link(v.tensor_tensor(y, t, y, ALU.mult))


def setup(nc, sb, sem, args, T):
    ld, done = sem("const_loaded"), sem("split_done")
    loads = [sem(f"weights_loaded{i}") for i in range(5)]
    T["experts_loaded"] = sem("experts_loaded")
    part, ones = sem("hi_part_done"), sem("ones_done")
    with nc.Block() as block:
        @block.sync
        def _(sp):
            sp.dma_start(T["consts"][:], args["consts"]).then_inc(ld, 16)
            sp.dma_start(T["wall"][:], args["wall"]).then_inc(loads[0], 16)
            sp.dma_start(T["rw"][:], args["rw"]).then_inc(loads[1], 16)
            sp.dma_start(T["wo"][:], args["wo"]).then_inc(loads[2], 16)
            sp.dma_start(T["cos"][:], args["cos"]).then_inc(loads[3], 16)
            sp.dma_start(T["sin"][:], args["sin"]).then_inc(loads[4], 16)
            sp.wait_ge(ld, 16)
            for s in loads:
                sp.wait_ge(s, 16)
            sp.dma_start(T["experts"][:, 0:E * 2 * F], args["gu"]).then_inc(T["experts_loaded"], 16)
            sp.dma_start(T["experts"][:, E * 2 * F:], args["dp"]).then_inc(T["experts_loaded"], 16)

        @block.scalar
        def _(act):
            act.wait_ge(loads[0], 16)
            act.activation(T["wall_hi"][:], T["wall"][:], ACT.Copy).then_inc(part, 1)

        @block.gpsimd
        def _(pool):
            for n in range(2):
                pool.memset(T["v32"][n][:, :, :, HD:HA], 1.0).then_inc(ones, 1)
                pool.memset(T["v_hi"][n][:, :, :, HD:HA], 1.0).then_inc(ones, 1)
                pool.memset(T["v_lo"][n][:, :, :, HD:HA], 0.0).then_inc(ones, 1)
            pool.memset(T["minus_half"][:], -0.5).then_inc(ones, 1)
            pool.wait_ge(ones, 7)

        @block.vector
        def _(dve):
            for n in ("rw_hi", "rw_lo"):
                dve.memset(T[n][:].bitcast(F32), 0.0).then_inc(done, 1)
            dve.wait_ge(loads[1], 16)
            dve.wait_ge(done, 2)
            dve.tensor_copy(T["rw_hi"][:, 0:E], T["rw"][:]).then_inc(done, 1)
            dve.wait_ge(done, 3)
            dve.tensor_tensor(T["rw_lo"][:, 0:E], T["rw"][:], T["rw_hi"][:, 0:E].bitcast(F32),
                              ALU.subtract).then_inc(done, 1)
            dve.wait_ge(part, 1)
            dve.tensor_tensor(T["wall_lo"][:], T["wall"][:], T["wall_hi"][:].bitcast(F32),
                              ALU.subtract).then_inc(done, 1)
            dve.wait_ge(ld, 16)
            dve.tensor_copy(T["sel"][:], T["consts"][0:2 * E, C_SEL:]).then_inc(done, 1)
            dve.wait_ge(done, 6)


def attention(nc, st, sb, ps, sem, args, T):
    con = T["consts"]
    ident = con[:, C_ID:C_ID + P]
    tri = con[:, C_TRI:C_TRI + P].rearrange("p (o i) -> p o i", o=1).broadcast_to([P, 4, P])
    par_mask = [con[:, C_EVEN:C_EVEN + 1], con[:, C_ODD:C_ODD + 1]]

    xT = [sb(f"xT{i}", [P, 2 * P], F32) for i in range(2)]
    xT_hi = [sb(f"xT_hi{i}", [P, 2 * P], F32R) for i in range(2)]
    xT_lo = [sb(f"xT_lo{i}", [P, 2 * P], F32R) for i in range(2)]
    x_tok = [sb(f"x_tok{i}", [P, 4, D], F32) for i in range(2)]
    rot_a, rot_b = sb("rot_a", [P, 4 * D], F32), sb("rot_b", [P, 4 * D], F32)
    qk_tok = [sb(f"qk_tok{i}", [P, 2, 2 * D], F32) for i in range(2)]
    v32, v_hi, v_lo = T["v32"], T["v_hi"], T["v_lo"]
    gate = [sb(f"gate{i}", [P, 4, V], F32) for i in range(2)]
    q32 = [sb(f"q32_{i}", [P, 2, P], F32) for i in range(2)]
    q_hi = [sb(f"q_hi{i}", [P, 2, 2, P], F32R) for i in range(2)]
    q_lo = [sb(f"q_lo{i}", [P, 2, 2, P], F32R) for i in range(2)]
    k_hi = [sb(f"k_hi{i}", [P, 2, P], F32R) for i in range(2)]
    k_lo = [sb(f"k_lo{i}", [P, 2, P], F32R) for i in range(2)]
    s32 = [sb(f"s32_{g}", [P, 4 * P], F32) for g in range(4)]
    s_hi = [sb(f"s_hi{g}", [P, 4 * P], BF16) for g in range(4)]
    s_lo = [sb(f"s_lo{g}", [P, 4 * P], BF16) for g in range(4)]
    state = [sb(f"state{i}", [P, H * HA], F32) for i in range(2)]
    kv_masked = sb("kv_masked", [P, H * HA], F32)
    o_sb = [sb(f"o_sb{i}", [P, 4, H, HA], F32) for i in range(2)]
    o_sq = [sb(f"o_sq{i}", [P, H, HD], F32) for i in range(2)]
    o_ms = [sb(f"o_ms{i}", [P, 4, H], F32) for i in range(2)]
    rms_v, rms_t = sb("rms_v", [P, 4 * H], F32), sb("rms_t", [P, 4 * H], F32)
    rms_r = sb("rms_r", [P, 4 * H], F32)
    gated = sb("gated", [P, 4, V], F32)
    gT = sb("gT", [P, 4, 2, P], F32)
    resid = sb("resid", [P, 4, D], F32)
    ln_st, ln_mv = sb("ln_st", [P, 4, 6], F32), sb("ln_mv", [P, 4, 2], F32)
    ln_v, ln_t, ln_r = (sb(f"ln_{c}", [P, 4], F32) for c in "vtr")
    h1 = sb("h1", [P, 4, D], F32)
    lgT = sb("lgT", [P, GT], F32)

    ps_s = [ps(f"ps_s{g}", [P, 4 * P]) for g in range(4)]
    ps_o, ps_vg, ps_qk, ps_t = ps("ps_o", [P, 4 * P]), ps("ps_vg", [P, 4 * P]), ps("ps_qk", [P, 4 * P]), ps("ps_t", [P, 4 * P])

    xT_loaded = [sem(f"xT_loaded{i}") for i in range(2)]
    x_tok_loaded = [sem(f"x_tok_loaded{i}") for i in range(2)]
    xhi_done, xlo_done = sem("xhi_done"), sem("xlo_done")
    qk_proj, vg_proj = sem("qk_proj"), sem("vg_proj")
    rope_done, qktok_done, qkT_done = sem("rope_done"), sem("qktok_done"), sem("qkT_done")
    qkhi_done, qklo_done = sem("qkhi_done"), sem("qklo_done")
    v_done, vlo_done = sem("v_done"), sem("vlo_done")
    scores_done, s32_done = sem("scores_done"), sem("s32_done")
    shi_done, slo_done = sem("shi_done"), sem("slo_done")
    kv_done, kv_read, state_done = sem("kv_done"), sem("kv_read"), sem("state_done")
    o_done, osb_done, ms_done = sem("o_done"), sem("osb_done"), sem("ms_done")
    rms_chain, gate_done, gated_done = sem("rms_chain"), sem("gate_done"), sem("gated_done")
    gT_done, gT_read, wo_done = sem("gT_done"), sem("gT_read"), sem("wo_done")
    ln_chain, h1T_done = sem("ln_chain"), sem("h1T_done")
    h1hi_done, h1lo_done = sem("h1hi_done"), sem("h1lo_done")
    lgT_done, lgT_read, lg_done, lg_read = sem("lgT_done"), sem("lgT_read"), sem("lg_done"), sem("lg_read")
    RMS_LINKS = 3 + NEWTON_LINKS + 1
    LN_LINKS = 1 + 4 + 6 + NEWTON_LINKS + 4

    def steps(eng, body):
        for pp in range(-2, PAIRS):
            body(0, pp)
        with eng.Fori(1, B - 1) as b:
            for pp in range(PAIRS):
                body(b, pp)
        for pp in range(PAIRS):
            body(B - 1, pp)
        for pp in range(3):
            body(B, pp)

    def kv_before(b, pp):
        return (POS - 1) * b + 2 * max(pp, 0)

    with nc.Block() as block:
        @block.sync
        def _(sp):
            def body(b, pp):
                n = PAIRS * b + pp
                if within(n + 2, NPAIR):
                    i = pp % 2
                    wait(sp, xhi_done, n + 1)
                    wait(sp, xlo_done, n + 1)
                    sp.dma_start(xT[i][:], args["xT"][:, ds((n + 2) * 2 * P, 2 * P)]).then_inc(xT_loaded[i], 16)
                if within(n, NPAIR) and pp % 2 == 0:
                    g = 2 * b + pp // 2
                    wait(sp, ln_chain, LN_LINKS * (g - 2) + 1)
                    sp.dma_start(x_tok[pp // 2 % 2][:],
                                 args["x"][ds(g * GT, GT), :].rearrange("(c p) d -> p c d", p=P)
                                 ).then_inc(x_tok_loaded[pp // 2 % 2], 16)
            steps(sp, body)

        @block.tensor
        def _(pe):
            def three_pass(out, w_hi, w_lo, x_hi, x_lo, first=True, last=True):
                pe.matmul(out, w_hi, x_hi, start=first, stop=False)
                pe.matmul(out, w_hi, x_lo, start=False, stop=False)
                return pe.matmul(out, w_lo, x_hi, start=False, stop=last)

            def project_vg(n, i, c):
                x = slice(c * P, (c + 1) * P)
                three_pass(ps_vg[:], xT_hi[i][:, x], xT_lo[i][:, x], T["wall_hi"][:, 2 * D:],
                           T["wall_lo"][:, 2 * D:]).then_inc(vg_proj, 1)

            def body(b, pp):
                n = PAIRS * b + pp
                i, j = pp % 2, (pp + 1) % 2
                main, front = within(n, NPAIR), within(n + 1, NPAIR)
                router_of = 2 * b + pp // 2 - 2 if pp % 2 == 0 else -1
                if front:
                    pe.wait_ge(xhi_done, n + 2)
                    pe.wait_ge(xlo_done, n + 2)
                    wait(pe, qkhi_done, 4 * (n + 1))
                    wait(pe, qklo_done, 3 * (n + 1))
                    for c in range(2):
                        x = slice(c * P, (c + 1) * P)
                        mm = three_pass(ps_qk[:, c * 2 * D:(c + 1) * 2 * D], xT_hi[j][:, x], xT_lo[j][:, x],
                                        T["wall_hi"][:, 0:2 * D], T["wall_lo"][:, 0:2 * D])
                    mm.then_inc(qk_proj, 1)
                    wait(pe, kv_read, kv_before(b, pp))
                    project_vg(n + 1, j, 0)
                if main:
                    for g in range(4):
                        wait(pe, s32_done, 4 * (n - 1) + g + 1)
                        rows = slice(32 * g, 32 * g + 32)
                        for c in range(2):
                            mm = three_pass(ps_s[g][:, c * 2 * P:(c + 1) * 2 * P], k_hi[i][rows, c, :],
                                            k_lo[i][rows, c, :], q_hi[i][rows, c, :, :], q_lo[i][rows, c, :, :])
                        mm.then_inc(scores_done, 1)
                if within(router_of, GROUPS):
                    pe.wait_ge(h1hi_done, router_of + 1)
                    pe.wait_ge(h1lo_done, router_of + 1)
                    at = ds(router_of * GT, GT)
                    three_pass(ps_t[:], T["rw_hi"][:], T["rw_lo"][:], T["h1T_hi"][:, at],
                               T["h1T_lo"][:, at]).then_inc(lgT_done, 1)
                if front:
                    pe.wait_ge(v_done, 6 * (n + 1) + 3)
                    project_vg(n + 1, j, 1)
                    pe.wait_ge(qktok_done, n + 2)
                    for k in range(4):
                        mm = pe.transpose(ps_qk[:, k * P:(k + 1) * P],
                                          qk_tok[j][:, k % 2, (k // 2) * D:(k // 2 + 1) * D], ident)
                    mm.then_inc(qkT_done, 1)
                if within(router_of, GROUPS):
                    pe.wait_ge(lgT_read, router_of + 1)
                    for c in range(4):
                        mm = pe.transpose(ps_t[:, c * P:(c + 1) * P], lgT[:, c * P:(c + 1) * P], ident)
                    mm.then_inc(lg_done, 1)
                if main:
                    for c in range(2):
                        pos = 2 * pp + c
                        m = 2 * n + c
                        if c == 0 and front:
                            pe.wait_ge(v_done, 6 * (n + 2))
                        if pos < POS - 1:
                            if c == 1 or not front:
                                pe.wait_ge(kv_read, (POS - 1) * b + pos)
                            pe.matmul(ps_vg[:, 0:H * HA], qk_tok[i][:, c, D:2 * D],
                                      v32[i][:, c, :, :].rearrange("p h a -> p (h a)"),
                                      start=True, stop=True).then_inc(kv_done, 1)
                        if c == 0:
                            pe.wait_ge(shi_done, 4 * n + 4)
                            pe.wait_ge(slo_done, 4 * n + 4)
                        pe.wait_ge(vlo_done, m + 1)
                        wait(pe, osb_done, 2 * m)
                        for h in range(H):
                            cols = slice((2 * c + h % 2) * P, (2 * c + h % 2 + 1) * P)
                            o = ps_o[:, h * HA:(h + 1) * HA]
                            for k, (s, v) in enumerate(((s_hi, v_hi), (s_hi, v_lo), (s_lo, v_hi))):
                                mm = pe.matmul(o, s[h // 2][:, cols], v[i][:, c, h, :], start=(h == 0 and k == 0),
                                               stop=(pos == 0), skip_group_check=True)
                        if pos:
                            if pos == 1:
                                pe.wait_ge(kv_read, (POS - 1) * b + 1)
                            else:
                                pe.wait_ge(state_done, (POS - 2) * b + pos - 1)
                            mm = pe.matmul(ps_o[:, 0:H * HA], q32[i][:, c, :], state[pos % 2][:],
                                           start=False, stop=True, skip_group_check=True)
                        mm.then_inc(o_done, 1)
                if pp % 2 == 0 and within(2 * b + pp // 2 - 1, GROUPS):
                    g = 2 * b + pp // 2 - 1
                    pe.wait_ge(gated_done, g + 1)
                    for half in range(2):
                        if half == 0:
                            wait(pe, lg_read, g)
                        else:
                            pe.wait_ge(gT_read, 2 * g + 1)
                        for k in range(4):
                            mm = pe.transpose(ps_t[:, k * P:(k + 1) * P],
                                              gated[:, 2 * half + k // 2, (k % 2) * P:(k % 2 + 1) * P], ident)
                        mm.then_inc(gT_done, 1)
                    pe.wait_ge(gT_read, 2 * g + 2)
                    for c in range(4):
                        for k in range(2):
                            mm = pe.matmul(ps_t[:, c * P:(c + 1) * P], gT[:, c, k, :], T["wo"][:, k * D:(k + 1) * D],
                                           start=(k == 0), stop=(k == 1))
                    mm.then_inc(wo_done, 1)
                if pp % 2 == 1 and within(2 * b + pp // 2 - 1, GROUPS):
                    g = 2 * b + pp // 2 - 1
                    pe.wait_ge(ln_chain, LN_LINKS * (g + 1))
                    for c in range(4):
                        mm = pe.transpose(ps_t[:, c * P:(c + 1) * P], h1[:, c, :], ident)
                    mm.then_inc(h1T_done, 1)
            steps(pe, body)

        @block.scalar
        def _(act):
            def read_vg(b, pp, j, c):
                n = PAIRS * b + pp
                act.wait_ge(vg_proj, 2 * (n + 1) + c + 1)
                if c == 0:
                    wait(act, o_done, 2 * n)
                    wait(act, vlo_done, 2 * n)
                v = ps_vg[:, 0:V].rearrange("p (h d) -> p h d", d=HD)
                act.activation(v32[j][:, c, :, 0:HD], v, ACT.Copy).then_inc(v_done, 1)
                act.activation(v_hi[j][:, c, :, 0:HD], v, ACT.Copy).then_inc(v_done, 1)
                wait(act, gated_done, 2 * b + (pp + 1) // 2 - 1)
                act.activation(gate[(pp + 1) // 2 % 2][:, 2 * j + c, :], ps_vg[:, V:2 * V], ACT.Silu
                               ).then_inc(v_done, 1)

            def body(b, pp):
                n = PAIRS * b + pp
                i, j = pp % 2, (pp + 1) % 2
                main, front = within(n, NPAIR), within(n + 1, NPAIR)
                router_of = 2 * b + pp // 2 - 2 if pp % 2 == 0 else -1
                if within(n + 2, NPAIR):
                    act.wait_ge(xT_loaded[i], 16 * (2 * b + (pp + 2) // 2 + 1))
                    wait(act, vg_proj, 2 * (n + 1))
                    wait(act, xlo_done, n + 1)
                    act.activation(xT_hi[i][:], xT[i][:], ACT.Copy).then_inc(xhi_done, 1)
                if front:
                    read_vg(b, pp, j, 0)
                if main:
                    wait(act, o_done, 2 * n)
                    for g in range(4):
                        act.wait_ge(s32_done, 4 * n + g + 1)
                        act.activation(s_hi[g][:], s32[g][:], ACT.Copy).then_inc(shi_done, 1)
                if front:
                    read_vg(b, pp, j, 1)
                if within(router_of, GROUPS):
                    act.wait_ge(lgT_done, router_of + 1)
                    wait(act, lg_done, router_of)
                    act.activation(lgT[:], ps_t[:], ACT.Copy).then_inc(lgT_read, 1)
                if front:
                    act.wait_ge(qkT_done, n + 2)
                    q = ps_qk[:, 0:2 * P].rearrange("p (c i) -> p c i", c=2)
                    k = ps_qk[:, 2 * P:].rearrange("p (c i) -> p c i", c=2)
                    act.activation(q32[j][:], q, ACT.Copy).then_inc(qkhi_done, 1)
                    for par in range(2):
                        act.activation(q_hi[j][:, :, par, :], q, ACT.Copy, scale=par_mask[par]).then_inc(qkhi_done, 1)
                    act.activation(k_hi[j][:], k, ACT.Copy).then_inc(qkhi_done, 1)
                if within(router_of, GROUPS):
                    act.wait_ge(lg_done, router_of + 1)
                    act.activation(T["logits"][:, ds(router_of * 4 * E, 4 * E)].rearrange("p (c e) -> p c e", e=E),
                                   ps_t[:].rearrange("p (c e) -> p c e", e=P)[:, :, 0:E], ACT.Copy).then_inc(lg_read, 1)
                if main:
                    if pp % 2 == 0:
                        wait(act, gated_done, 2 * b + pp // 2 - 1)
                    for c in range(2):
                        m = 2 * n + c
                        act.wait_ge(o_done, m + 1)
                        o = ps_o[:, 0:H * HA].rearrange("p (h a) -> p h a", a=HA)
                        act.activation(o_sb[pp // 2 % 2][:, 2 * i + c, :, :], o, ACT.Copy).then_inc(osb_done, 1)
                        wait(act, ms_done, m - 1)
                        act.activation(o_sq[c][:], o[:, :, 0:HD], ACT.Square).then_inc(osb_done, 1)
                if pp % 2 == 0 and within(2 * b + pp // 2 - 1, GROUPS):
                    g = 2 * b + pp // 2 - 1
                    wait(act, wo_done, g)
                    for half in range(2):
                        act.wait_ge(gT_done, 2 * g + half + 1)
                        act.activation(gT[:, 2 * half:2 * half + 2, :, :],
                                       ps_t[:].rearrange("p (c k i) -> p c k i", c=2, k=2), ACT.Copy
                                       ).then_inc(gT_read, 1)
                if pp % 2 == 1 and within(2 * b + pp // 2 - 1, GROUPS):
                    g = 2 * b + pp // 2 - 1
                    act.wait_ge(h1T_done, g + 1)
                    act.activation(T["h1T_hi"][:, ds(g * GT, GT)], ps_t[:], ACT.Copy).then_inc(h1hi_done, 1)
            steps(act, body)

        @block.gpsimd
        def _(pool):
            def v_lower(n, j, c):
                pool.wait_ge(v_done, 6 * (n + 1) + 3 * c + 2)
                pool.tensor_tensor(v_lo[j][:, c, :, 0:HD], v32[j][:, c, :, 0:HD], v_hi[j][:, c, :, 0:HD],
                                   ALU.subtract).then_inc(vlo_done, 1)

            def body(b, pp):
                n = PAIRS * b + pp
                i, j = pp % 2, (pp + 1) % 2
                main, front = within(n, NPAIR), within(n + 1, NPAIR)
                if within(n + 2, NPAIR):
                    pool.wait_ge(xhi_done, n + 3)
                    pool.tensor_tensor(xT_lo[i][:], xT[i][:], xT_hi[i][:].bitcast(F32), ALU.subtract
                                       ).then_inc(xlo_done, 1)
                if front:
                    pool.wait_ge(rope_done, 2 * (n + 2))
                    wait(pool, o_done, 2 * n)
                    pool.tensor_tensor(qk_tok[j][:].rearrange("p c d -> p (c d)"), rot_a[:], rot_b[:], ALU.add
                                       ).then_inc(qktok_done, 1)
                    v_lower(n, j, 0)
                if main:
                    wait(pool, o_done, 2 * n)
                    for g in range(4):
                        pool.wait_ge(shi_done, 4 * n + g + 1)
                        pool.tensor_tensor(s_lo[g][:], s32[g][:], s_hi[g][:], ALU.subtract).then_inc(slo_done, 1)
                if front:
                    v_lower(n, j, 1)
                if main and pp % 2 == 1:
                    g = 2 * b + pp // 2
                    pool.wait_ge(rms_chain, RMS_LINKS * (g + 1))
                    pool.wait_ge(v_done, 6 * (n + 1))
                    r = rms_r[:].rearrange("p (h o) -> p h o", o=1).broadcast_to([P, 4 * H, HD])
                    scaled = gate[pp // 2 % 2][:].rearrange("p c (h d) -> p (c h) d", d=HD)
                    pool.tensor_tensor(scaled, scaled, r, ALU.mult).then_inc(gate_done, 1)
            steps(pool, body)

        @block.vector
        def _(dve):
            def body(b, pp):
                n = PAIRS * b + pp
                i, j = pp % 2, (pp + 1) % 2
                main, front = within(n, NPAIR), within(n + 1, NPAIR)
                if front:
                    dve.wait_ge(qk_proj, n + 2)
                    wait(dve, qktok_done, n + 1)
                    at = slice((pp + 1) % PAIRS * 4 * D, ((pp + 1) % PAIRS + 1) * 4 * D)
                    two = "p (d t) -> p d t"
                    dve.tensor_tensor(rot_a[:], ps_qk[:], T["cos"][:, at], ALU.mult).then_inc(rope_done, 1)
                    dve.tensor_tensor(rot_b[:].rearrange(two, t=2), ps_qk[:].rearrange(two, t=2)[:, :, ::-1],
                                      T["sin"][:, at].rearrange(two, t=2), ALU.mult).then_inc(rope_done, 1)
                if pp % 2 == 0 and within(2 * b + pp // 2 - 1, GROUPS):
                    g = 2 * b + pp // 2 - 1
                    dve.wait_ge(gate_done, g + 1)
                    wait(dve, gT_done, 2 * g)
                    dve.tensor_tensor(gated[:].rearrange("p c (h d) -> p c h d", d=HD),
                                      o_sb[(pp // 2 - 1) % 2][:, :, :, 0:HD],
                                      gate[(pp // 2 - 1) % 2][:].rearrange("p c (h d) -> p c h d", d=HD), ALU.mult
                                      ).then_inc(gated_done, 1)
                if main:
                    for g in range(4):
                        dve.wait_ge(scores_done, 4 * n + g + 1)
                        wait(dve, slo_done, 4 * (n - 1) + g + 1)
                        dve.tensor_tensor(s32[g][:].rearrange("p (r i) -> p r i", i=P),
                                          ps_s[g][:].rearrange("p (r i) -> p r i", i=P), tri, ALU.mult
                                          ).then_inc(s32_done, 1)
                if front:
                    dve.wait_ge(qkhi_done, 4 * (n + 2))
                    q = ps_qk[:, 0:2 * P].rearrange("p (c i) -> p c i", c=2)
                    k = ps_qk[:, 2 * P:].rearrange("p (c i) -> p c i", c=2)
                    for par in range(2):
                        dve.scalar_tensor_tensor(out=q_lo[j][:, :, par, :], in0=q, scalar=par_mask[par],
                                                 in1=q_hi[j][:, :, par, :].bitcast(F32), op0=ALU.mult,
                                                 op1=ALU.subtract).then_inc(qklo_done, 1)
                    dve.tensor_tensor(k_lo[j][:], k, k_hi[j][:].bitcast(F32), ALU.subtract).then_inc(qklo_done, 1)
                if main:
                    for c in range(2):
                        pos, m = 2 * pp + c, 2 * n + c
                        if pos < POS - 1:
                            dve.wait_ge(kv_done, (POS - 1) * b + pos + 1)
                            wait(dve, o_done, m)
                            wait(dve, state_done, (POS - 2) * b + max(pos - 1, 0))
                            out = state[1] if pos == 0 else kv_masked
                            dve.tensor_tensor(out[:], ps_vg[:, 0:H * HA], con[:, C_DECAY:C_GAMMA], ALU.mult
                                              ).then_inc(kv_read, 1)
                            if pos:
                                dve.wait_ge(kv_read, (POS - 1) * b + pos + 1)
                                dve.scalar_tensor_tensor(out=state[(pos + 1) % 2][:], in0=state[pos % 2][:],
                                                         scalar=con[:, C_GAMMA:C_GAMMA + 1], in1=kv_masked[:],
                                                         op0=ALU.mult, op1=ALU.add).then_inc(state_done, 1)
                        dve.wait_ge(osb_done, 2 * (m + 1))
                        dve.tensor_reduce(o_ms[pp // 2 % 2][:, 2 * i + c, :], o_sq[c][:], AX_X, ALU.add
                                          ).then_inc(ms_done, 1)
                if main and pp % 2 == 1:
                    g = 2 * b + pp // 2
                    link = Chain(dve, rms_chain, RMS_LINKS * g)
                    dve.wait_ge(ms_done, 4 * (g + 1))
                    wait(dve, gate_done, g)
                    v = rms_v[:].rearrange("p (c h) -> p c h", h=H)
                    total = o_sb[pp // 2 % 2][:, :, :, HD]
                    guard = con[:, C_GUARD + pp // 2 * 4 * H:C_GUARD + (pp // 2 + 1) * 4 * H]
                    link(dve.scalar_tensor_tensor(out=v, in0=total, scalar=HD * EPS, in1=total,
                                                  op0=ALU.mult, op1=ALU.mult))
                    link(dve.tensor_tensor(rms_v[:], rms_v[:], guard, ALU.max))
                    link(dve.tensor_tensor(v, v, o_ms[pp // 2 % 2][:], ALU.add))
                    newton_rsqrt(dve, link, rms_v[:], rms_r[:], rms_t[:], float(HD) ** 0.5)
                    assert link.n == RMS_LINKS
                if pp % 2 == 0 and within(2 * b + pp // 2 - 1, GROUPS):
                    g = 2 * b + pp // 2 - 1
                    link = Chain(dve, ln_chain, LN_LINKS * g)
                    dve.wait_ge(wo_done, g + 1)
                    dve.wait_ge(x_tok_loaded[(pp // 2 - 1) % 2], 16 * (b + (pp // 2 - 1) // 2 + 1))
                    link(dve.tensor_tensor(resid[:].rearrange("p c d -> p (c d)"), ps_t[:],
                                           x_tok[(pp // 2 - 1) % 2][:].rearrange("p c d -> p (c d)"), ALU.add))
                    wait(dve, h1T_done, g)
                    layernorm(dve, link, [resid[:, c, :] for c in range(4)], ln_st, ln_mv, ln_v, ln_t, ln_r,
                              [h1[:, c, :] for c in range(4)])
                    assert link.n == LN_LINKS, link.n
                if pp % 2 == 1 and within(2 * b + pp // 2 - 1, GROUPS):
                    g = 2 * b + pp // 2 - 1
                    dve.wait_ge(h1hi_done, g + 1)
                    at = ds(g * GT, GT)
                    dve.tensor_tensor(T["h1T_lo"][:, at], ps_t[:], T["h1T_hi"][:, at].bitcast(F32), ALU.subtract
                                      ).then_inc(h1lo_done, 1)
            steps(dve, body)


LN_STATS, LN_COMBINE, LN_APPLY = 4, 6, 4


def layernorm_stats(dve, chain, rows, stats):
    for c, x in enumerate(rows):
        chain.step(dve.bn_stats(out=stats[:, c, :], in_=x))


def layernorm_combine(dve, chain, stats, mv, v, t):
    mean, half = mv[:, :, 0], mv[:, :, 1]
    chain.wait()
    chain.step(dve.scalar_tensor_tensor(out=v[:], in0=stats[:, :, 2], scalar=D * EPS, in1=stats[:, :, 5],
                                        op0=ALU.add, op1=ALU.add))
    chain.step(dve.tensor_tensor(mean, stats[:, :, 1], stats[:, :, 4], ALU.add))
    chain(dve.tensor_tensor(half, stats[:, :, 1], stats[:, :, 4], ALU.subtract))
    chain.step(dve.scalar_tensor_tensor(out=t[:], in0=half, scalar=0.25, in1=half, op0=ALU.mult, op1=ALU.mult))
    chain(dve.tensor_scalar(mean, mean, 0.5, None, ALU.mult))
    chain.step(dve.scalar_tensor_tensor(out=v[:], in0=v[:], scalar=1.0 / D, in1=t[:], op0=ALU.mult, op1=ALU.add))


def layernorm_apply(dve, chain, rows, mv, r, outs):
    for c, x in enumerate(rows):
        chain.step(dve.tensor_scalar(outs[c], x, mv[:, c, 0:1], r[:, c:c + 1], ALU.subtract, ALU.mult))


def layernorm(dve, link, rows, stats, mv, v, t, r, outs):
    layernorm_stats(dve, link, rows, stats)
    layernorm_combine(dve, link, stats, mv, v, t)
    link.wait()
    newton_rsqrt(dve, link, v[:], r[:], t[:], 1.0)
    layernorm_apply(dve, link, rows, mv, r, outs)


def routing(nc, sb, ps, sem, T):
    W = NCH * E
    lg = T["logits"]
    con = T["consts"]
    by = "p (n e) -> p n e"
    hot1, hot2, tmp, left = (sb(n, [P, W], F32) for n in ("hot1", "hot2", "tmp", "left"))
    top1, top2, at, gap, ratio, den, w1, w2 = (sb(n, [P, NCH], F32) for n in (
        "top1", "top2", "at", "gap", "ratio", "den", "w1", "w2"))
    wts = sb("wts", [P, W], F32)
    parts = sb("parts", [P, NCH, 2 * E], F32R)
    banks = [ps(f"ps_w{n}", [2 * E, GT]) for n in range(8)]
    chain, exp_done, parts_done = sem("routing_chain"), sem("exp_done"), sem("parts_done")
    tr_done, read_even, read_odd = sem("weights_transposed"), sem("read_even"), sem("read_odd")
    ehi, elo = sem("experts_hi_done"), sem("experts_lo_done")
    idx = con[:, C_IDX:C_IDX + E].rearrange("p (o e) -> p o e", o=1).broadcast_to([P, NCH, E])

    def each(col):
        return col[:].rearrange("p (n o) -> p n o", o=1).broadcast_to([P, NCH, E])

    def table(t):
        return t[:].rearrange(by, e=E)

    QUARTER = E * 3 * F // 4
    with nc.Block() as block:
        @block.vector
        def _(dve):
            link = Chain(dve, chain, 0)
            scores = lg
            for top, hot in ((top1, hot1), (top2, hot2)):
                link(dve.tensor_reduce(top[:], table(scores), AX_X, ALU.max))
                link(dve.tensor_tensor(table(tmp), table(scores), each(top), ALU.is_equal))
                link(dve.tensor_tensor(table(tmp), table(tmp), idx, ALU.mult))
                link(dve.tensor_reduce(at[:], table(tmp), AX_X, ALU.max))
                link(dve.tensor_tensor(table(hot), idx, each(at), ALU.is_equal))
                if top is top1:
                    link(dve.scalar_tensor_tensor(out=left[:], in0=hot[:], scalar=-3.0e38, in1=lg[:],
                                                  op0=ALU.mult, op1=ALU.add))
                    scores = left
            link(dve.tensor_tensor(gap[:], top2[:], top1[:], ALU.subtract))
            dve.wait_ge(exp_done, 1)
            link(dve.tensor_scalar(den[:], ratio[:], 1.0, None, ALU.add))
            link(dve.reciprocal(w1[:], den[:]))
            link(dve.tensor_tensor(w2[:], ratio[:], w1[:], ALU.mult))
            link(dve.tensor_tensor(table(hot1), table(hot1), each(w1), ALU.mult))
            link(dve.tensor_tensor(table(hot2), table(hot2), each(w2), ALU.mult))
            link(dve.tensor_tensor(wts[:], hot1[:], hot2[:], ALU.add))
            link(dve.tensor_copy(parts[:, :, 0:E], table(wts)))
            dve.tensor_tensor(parts[:, :, E:2 * E], table(wts), parts[:, :, 0:E].bitcast(F32), ALU.subtract
                              ).then_inc(parts_done, 1)
            for g in range(1, GROUPS, 2):
                dve.wait_ge(tr_done, g + 1)
                dve.tensor_copy(T["wT"][:, g * GT:(g + 1) * GT], banks[g % 8][:]).then_inc(read_odd, 1)
            dve.wait_ge(read_odd, GROUPS // 2)

        @block.scalar
        def _(act):
            act.wait_ge(T["experts_loaded"], 32)
            for n in range(4):
                part = slice(n * QUARTER, (n + 1) * QUARTER)
                act.activation(T["experts_hi"][:, part], T["experts"][:, part], ACT.Copy).then_inc(ehi, 1)
            act.wait_ge(chain, 12)
            act.activation(ratio[:], gap[:], ACT.Exp).then_inc(exp_done, 1)
            for g in range(0, GROUPS, 2):
                act.wait_ge(tr_done, g + 1)
                act.activation(T["wT"][:, g * GT:(g + 1) * GT], banks[g % 8][:], ACT.Copy).then_inc(read_even, 1)
            act.wait_ge(read_even, GROUPS // 2)

        @block.gpsimd
        def _(pool):
            for n in range(4):
                part = slice(n * QUARTER, (n + 1) * QUARTER)
                pool.wait_ge(ehi, n + 1)
                pool.tensor_tensor(T["experts_lo"][:, part], T["experts"][:, part],
                                   T["experts_hi"][:, part].bitcast(F32), ALU.subtract).then_inc(elo, 1)
            pool.wait_ge(elo, 4)

        @block.tensor
        def _(pe):
            pe.wait_ge(parts_done, 1)
            for g in range(GROUPS):
                wait(pe, read_odd if g % 2 else read_even, (g - 8) // 2 + 1)
                for c in range(4):
                    mm = pe.transpose(banks[g % 8][:, c * P:(c + 1) * P], parts[:, 4 * g + c, :].bitcast(F32),
                                      con[:, C_ID:C_ID + P])
                mm.then_inc(tr_done, 1)


def experts(nc, sb, ps, sem, args, T):
    con = T["consts"]
    ident = con[:, C_ID:C_ID + P]
    act_s = [sb(f"act_s{i}", [P, GT], F32) for i in range(2)]
    w_sb = [sb(f"w_sb{i}", [P, GT], F32) for i in range(2)]
    uw = sb("uw", [P, GT], F32)
    a32 = [sb(f"a32_{i}", [P, GT], F32) for i in range(2)]
    a_hi = [sb(f"a_hi{i}", [P, GT], F32R) for i in range(2)]
    a_lo = [sb(f"a_lo{i}", [P, GT], F32R) for i in range(2)]
    z1, z = sb("z1", [P, GT], F32), sb("z", [P, GT], F32)
    z_tok = sb("z_tok", [P, GT], F32)
    ln_st, ln_mv = sb("ln2_st", [P, 4, 6], F32), sb("ln2_mv", [P, 4, 2], F32)
    ln_v, ln_t, ln_r = (sb(f"ln2_{c}", [P, 4], F32) for c in "vtr")
    y = [sb(f"y{i}", [P, 4, D], F32) for i in range(2)]
    ps_gate = [ps(f"ps_gate{i}", [P, GT]) for i in range(2)]
    ps_up = [ps(f"ps_up{i}", [P, GT]) for i in range(2)]
    ps_w = [ps(f"ps_wt{i}", [P, GT]) for i in range(2)]
    ps_acc = [ps(f"ps_acc{i}", [P, GT]) for i in range(2)]

    gate_mm, w_mm, up_mm = sem("gate_mm"), sem("w_mm"), sem("up_mm")
    silu_done, wsb_done, uw_done, a_done = sem("silu_done"), sem("wsb_done"), sem("uw_done"), sem("a_done")
    ahi_done, alo_done, down_mm = sem("ahi_done"), sem("alo_done"), sem("down_mm")
    z1_done, z_done, zT_done, ztok_done = sem("z1_done"), sem("z_done"), sem("zT_done"), sem("ztok_done")
    ln_chain, ln_r_done = sem("ln2_chain"), sem("ln2_r_done")
    stored = [sem(f"stored{i}") for i in range(2)]
    LN_LINKS = LN_STATS + LN_COMBINE + LN_APPLY
    ROUND = 2 * E
    TURNS = GROUPS // 2
    STEPS = GROUPS * E

    def steps(eng, body, ahead):
        for k in range(-ahead, ROUND):
            body(0, k)
        with eng.Fori(1, TURNS - 1) as t:
            for k in range(ROUND):
                body(t, k)
        for k in range(ROUND):
            body(TURNS - 1, k)
        for k in range(5):
            body(TURNS, k)

    with nc.Block() as block:
        @block.tensor
        def _(pe):
            def three_pass(out, w_hi, w_lo, x_hi, x_lo, first=True, last=True):
                pe.matmul(out, w_hi, x_hi, start=first, stop=False)
                pe.matmul(out, w_lo, x_hi, start=False, stop=False)
                return pe.matmul(out, w_hi, x_lo, start=False, stop=last)

            def body(t, k):
                n = ROUND * t + k
                if within(n + 2, STEPS):
                    e, i = (k + 2) % E, k % 2
                    at = ds((2 * t + (k + 2) // E) * GT, GT)
                    hi, lo = T["experts_hi"], T["experts_lo"]
                    xh, xl = T["h1T_hi"][:, at], T["h1T_lo"][:, at]
                    g = slice(e * 2 * F, e * 2 * F + F)
                    u = slice(e * 2 * F + F, (e + 1) * 2 * F)
                    wait(pe, silu_done, n + 1)
                    wait(pe, wsb_done, n + 1)
                    three_pass(ps_gate[i][:], hi[:, g], lo[:, g], xh, xl).then_inc(gate_mm, 1)
                    pe.matmul(ps_w[i][:], T["sel"][:, e * P:(e + 1) * P], T["wT"][:, at], start=True, stop=True
                              ).then_inc(w_mm, 1)
                    wait(pe, uw_done, n + 1)
                    three_pass(ps_up[i][:], hi[:, u], lo[:, u], xh, xl).then_inc(up_mm, 1)
                if within(n, STEPS):
                    e, i = k % E, k % 2
                    w = slice(E * 2 * F + e * D, E * 2 * F + (e + 1) * D)
                    acc = ps_acc[k // E % 2][:]
                    pe.wait_ge(ahi_done, n + 1)
                    if e == 0:
                        wait(pe, ztok_done, 2 * t + k // E - 1)
                    hi, lo = T["experts_hi"], T["experts_lo"]
                    pe.matmul(acc, hi[:, w], a_hi[i][:], start=(e == 0), stop=False)
                    pe.matmul(acc, lo[:, w], a_hi[i][:], start=False, stop=False)
                    pe.wait_ge(alo_done, n + 1)
                    pe.matmul(acc, hi[:, w], a_lo[i][:], start=False, stop=(e == E - 1)).then_inc(down_mm, 1)
                done = 2 * t + k // E - 1
                if k % E == 1 and within(done, GROUPS):
                    pe.wait_ge(z_done, done + 1)
                    bank = ps_acc[(k // E - 1) % 2]
                    for c in range(4):
                        mm = pe.transpose(bank[:, c * P:(c + 1) * P], z[:, c * P:(c + 1) * P], ident)
                    mm.then_inc(zT_done, 1)
            steps(pe, body, 2)

        @block.scalar
        def _(act):
            def body(t, k):
                n = ROUND * t + k
                if within(n + 1, STEPS):
                    i = (k + 1) % 2
                    act.wait_ge(gate_mm, n + 2)
                    wait(act, a_done, n)
                    act.activation(act_s[i][:], ps_gate[i][:], ACT.Silu).then_inc(silu_done, 1)
                    act.wait_ge(w_mm, n + 2)
                    wait(act, uw_done, n)
                    act.activation(w_sb[i][:], ps_w[i][:], ACT.Copy).then_inc(wsb_done, 1)
                if within(n, STEPS):
                    i = k % 2
                    act.wait_ge(a_done, n + 1)
                    wait(act, down_mm, n - 1)
                    act.activation(a_hi[i][:], a32[i][:], ACT.Copy).then_inc(ahi_done, 1)
                done = 2 * t + k // E - 1
                if k % E == 1 and within(done, GROUPS):
                    act.wait_ge(zT_done, done + 1)
                    wait(act, ln_chain, LN_LINKS * done)
                    act.activation(z_tok[:], ps_acc[(k // E - 1) % 2][:], ACT.Copy).then_inc(ztok_done, 1)
            steps(act, body, 1)

        @block.gpsimd
        def _(pool):
            def body(t, k):
                n = ROUND * t + k
                if within(n, STEPS):
                    i = k % 2
                    pool.wait_ge(ahi_done, n + 1)
                    wait(pool, down_mm, n - 1)
                    pool.tensor_tensor(a_lo[i][:], a32[i][:], a_hi[i][:].bitcast(F32), ALU.subtract
                                       ).then_inc(alo_done, 1)
                done = 2 * t + k // E - 1
                if k % E == 3 and within(done, GROUPS):
                    pool.wait_ge(ln_chain, LN_LINKS * done + LN_STATS + LN_COMBINE)
                    pool.tensor_tensor(ln_r[:], ln_v[:], T["minus_half"][:], ALU.pow).then_inc(ln_r_done, 1)
            steps(pool, body, 0)

        @block.vector
        def _(dve):
            def body(t, k):
                n = ROUND * t + k
                if within(n, STEPS):
                    i = k % 2
                    dve.wait_ge(wsb_done, n + 1)
                    dve.wait_ge(up_mm, n + 1)
                    wait(dve, a_done, n)
                    dve.tensor_tensor(uw[:], w_sb[i][:], ps_up[i][:], ALU.mult).then_inc(uw_done, 1)
                    dve.wait_ge(uw_done, n + 1)
                    dve.wait_ge(silu_done, n + 1)
                    wait(dve, alo_done, n - 1)
                    dve.tensor_tensor(a32[i][:], act_s[i][:], uw[:], ALU.mult).then_inc(a_done, 1)
                done, i = 2 * t + k // E - 1, (k // E - 1) % 2
                if k % E == 0 and within(done, GROUPS):
                    at = ds(done * GT, GT)
                    dve.wait_ge(down_mm, E * (done + 1))
                    wait(dve, z_done, done)
                    dve.tensor_tensor(z1[:], ps_acc[i][:], T["h1T_hi"][:, at].bitcast(F32), ALU.add
                                      ).then_inc(z1_done, 1)
                    dve.wait_ge(z1_done, done + 1)
                    wait(dve, zT_done, done)
                    dve.tensor_tensor(z[:], z1[:], T["h1T_lo"][:, at].bitcast(F32), ALU.add).then_inc(z_done, 1)
                rows = [z_tok[:, c * P:(c + 1) * P] for c in range(4)]
                if k % E == 2 and within(done, GROUPS):
                    dve.wait_ge(ztok_done, done + 1)
                    layernorm_stats(dve, Chain(dve, ln_chain, LN_LINKS * done), rows, ln_st)
                if k % E == 3 and within(done, GROUPS):
                    wait(dve, ln_r_done, done)
                    layernorm_combine(dve, Chain(dve, ln_chain, LN_LINKS * done + LN_STATS), ln_st, ln_mv,
                                      ln_v, ln_t)
                if k % E == 4 and within(done, GROUPS):
                    dve.wait_ge(ln_chain, LN_LINKS * done + LN_STATS + LN_COMBINE)
                    dve.wait_ge(ln_r_done, done + 1)
                    wait(dve, stored[i], 16 * (t + (k // E - 1) // 2))
                    layernorm_apply(dve, Chain(dve, ln_chain, LN_LINKS * done + LN_STATS + LN_COMBINE), rows,
                                    ln_mv, ln_r, [y[i][:, c, :] for c in range(4)])
            steps(dve, body, 0)

        @block.sync
        def _(sp):
            def store(g, i):
                sp.wait_ge(ln_chain, LN_LINKS * (g + 1))
                sp.dma_start(args["out"][ds(g * GT, GT), :].rearrange("(c p) d -> p c d", p=P), y[i][:]
                             ).then_inc(stored[i], 16)
            with sp.Fori(0, TURNS) as t:
                for i in range(2):
                    store(2 * t + i, i)
            for i in range(2):
                sp.wait_ge(stored[i], 16 * TURNS)


def build(nc, args):
    T = {}
    with ExitStack() as keep:
        def pool_of(stack):
            def sb(name, shape, dt):
                return stack.enter_context(nc.sbuf_tensor(name, shape, dt))

            def ps(name, shape):
                return stack.enter_context(nc.psum_tensor(name, shape, F32))
            return sb, ps

        def sem(name):
            return keep.enter_context(nc.semaphore(name))

        sb, _ = pool_of(keep)
        T["consts"] = sb("consts", [P, C_END], F32)
        T["sel"] = sb("sel", [2 * E, E * P], F32R)
        T["experts"] = sb("experts", [P, E * 3 * F], F32)
        T["h1T_hi"] = sb("h1T_hi", [P, B * S], F32R)
        T["h1T_lo"] = sb("h1T_lo", [P, B * S], F32R)
        T["minus_half"] = sb("minus_half", [P, 4], F32)
        T["logits"] = sb("logits", [P, NCH * E], F32)
        with ExitStack() as own:
            sb, ps = pool_of(own)
            for n, w in (("wo", 2 * D), ("cos", POS * 2 * D), ("sin", POS * 2 * D)):
                T[n] = sb(n, [P, w], F32)
            T["wall_hi"], T["wall_lo"] = (sb(n, [P, 2 * D + 2 * V], F32R) for n in ("wall_hi", "wall_lo"))
            T["rw_hi"], T["rw_lo"] = (sb(n, [P, P], F32R) for n in ("rw_hi", "rw_lo"))
            for n, dt in (("v32", F32), ("v_hi", BF16), ("v_lo", BF16)):
                T[n] = [sb(f"{n}_{i}", [P, 2, H, HA], dt) for i in range(2)]
            with ExitStack() as staging:
                T["wall"] = pool_of(staging)[0]("wall", [P, 2 * D + 2 * V], F32)
                T["rw"] = pool_of(staging)[0]("rw", [P, E], F32)
                setup(nc, sb, sem, args, T)
            attention(nc, own, sb, ps, sem, args, T)
        T["wT"] = pool_of(keep)[0]("wT", [2 * E, B * S], F32R)
        T["experts_hi"] = pool_of(keep)[0]("experts_hi", [P, E * 3 * F], F32R)
        T["experts_lo"] = pool_of(keep)[0]("experts_lo", [P, E * 3 * F], F32R)
        with ExitStack() as own:
            routing(nc, *pool_of(own), sem, T)
        with ExitStack() as own:
            experts(nc, *pool_of(own), sem, args, T)


def kernel(**inputs):
    import concourse.bacc as bacc
    from concourse.bass_utils import run_bass_kernel_spmd

    consts, cos, sin = shape_constants()
    a = {k: np.asarray(v) for k, v in inputs.items()}
    x = a["L0_attn_x"].reshape(B * S, D)
    arrays = {
        "x": np.ascontiguousarray(x),
        "xT": np.ascontiguousarray(x.T),
        "wall": np.ascontiguousarray(np.concatenate([a["L0_attn_" + n] for n in ("wq", "wk", "wv", "wg")], axis=1)),
        "wo": np.ascontiguousarray(a["L0_attn_wo"].reshape(2, P, D).transpose(1, 0, 2).reshape(P, 2 * D)),
        "rw": np.ascontiguousarray(a["L0_ffn_router_weight"].T),
        "gu": np.ascontiguousarray(a["L0_ffn_gate_up_proj"].transpose(2, 0, 1).reshape(D, E * 2 * F)),
        "dp": np.ascontiguousarray(a["L0_ffn_down_proj"].transpose(2, 0, 1).reshape(F, E * D)),
        "consts": consts, "cos": cos, "sin": sin,
    }
    nc = bacc.Bacc("TRN2", target_bir_lowering=False, num_devices=1)
    args = {n: nc.dram_tensor(f"in_{n}", v.shape, mybir.dt.from_np(v.dtype), kind="ExternalInput").ap()
            for n, v in arrays.items()}
    args["out"] = nc.dram_tensor("out_y", (B * S, D), F32, kind="ExternalOutput").ap()
    build(nc, args)
    r = run_bass_kernel_spmd(nc, [{f"in_{n}": v for n, v in arrays.items()}], core_ids=[0])
    return r.results[0]["out_y"].reshape(B, S, D)
```

```python
from contextlib import ExitStack

import numpy as np
import concourse.bass as bass
from concourse import mybir

F32 = mybir.dt.float32
F32R = mybir.dt.float32r
BF16 = mybir.dt.bfloat16
I32 = mybir.dt.int32
ALU = mybir.AluOpType
ACT = mybir.ActivationFunctionType
AX_X = mybir.AxisListType.X
ds = bass.ds

B, S, D = 8, 1024, 128
H, KD, HD = 8, 16, 32
V = H * HD
HA = HD + 1
E, F = 8, 128
P = 128
POS = S // P
PAIRS = POS // 2
NPAIR = B * PAIRS
GROUPS = NPAIR // 2
GT = 4 * P
NCH = B * POS
EPS = 1e-5
RSQRT_MAGIC = float(0x5F3759DF)
NEWTON_LINKS = 2 + 3 * 3 + 1
LN_STATS, LN_COMBINE, LN_APPLY = 4, 6, 4

C_ID, C_TRI, C_DECAY = 0, 128, 256
C_GAMMA = C_DECAY + H * HA
C_EVEN, C_ODD = C_GAMMA + 1, C_GAMMA + 2
C_GUARD = C_ODD + 1
C_IDX = C_GUARD + POS * H
C_SEL = C_IDX + E
C_END = C_SEL + E * P


def shape_constants():
    c = np.zeros((P, C_END), np.float32)
    t = np.arange(P)
    decay = np.log1p(-2.0 ** (-5.0 - np.arange(H)))
    c[:, C_ID:C_ID + P] = np.eye(P)
    c[:, C_TRI:C_TRI + P] = t[:, None] <= t[None, :]
    head = t // KD
    block = (head[:, None] == np.arange(H)[None, :]) * np.exp(P * decay)[None, :]
    c[:, C_DECAY:C_GAMMA] = np.repeat(block, HA, axis=1)
    c[:, C_GAMMA] = np.exp(P * decay)[head]
    c[:, C_EVEN] = head % 2 == 0
    c[:, C_ODD] = head % 2 == 1
    i = np.arange(S)
    total = (1 - np.exp((i[:, None] + 1) * decay)) / (1 - np.exp(decay))
    guard = HD * EPS * total * np.exp(-2 * (i % P)[:, None] * decay)
    c[:, C_GUARD:C_IDX] = guard.reshape(POS, P, H).transpose(1, 0, 2).reshape(P, POS * H)
    c[:, C_IDX:C_SEL] = E - np.arange(E)
    sel = np.zeros((P, E, P))
    for e in range(E):
        sel[e, e] = sel[E + e, e] = 1
    c[:, C_SEL:] = sel.reshape(P, E * P)
    at = np.arange(KD // 2, dtype=np.float32) * np.float32(1 / (KD // 2 - 1))
    angle = np.repeat((1 / 10000.0 ** at.astype(np.float64)).astype(np.float32), 2)
    phase = (i.astype(np.float32)[:, None] * angle[None, :]).astype(np.float64)
    sign = np.where(np.arange(KD) % 2 == 0, -1.0, 1.0)
    kscale = KD ** -0.5 * np.exp(-(i % P)[:, None] * decay)
    out = []
    for table in (np.cos(phase), np.sin(phase) * sign):
        q = np.tile(table, (1, H))
        k = (kscale[:, :, None] * table[:, None, :]).reshape(S, H * KD)
        both = np.concatenate([q, k], axis=1).reshape(POS, P, 2 * D)
        out.append(both.transpose(1, 0, 2).reshape(P, POS * 2 * D).astype(np.float32))
    return c, out[0], out[1]


def wait(eng, sem, value):
    if isinstance(value, int) and value <= 0:
        return
    eng.wait_ge(sem, value)


def within(n, end):
    return not isinstance(n, int) or 0 <= n < end


class Chain:

    def __init__(self, eng, sem, base):
        self.eng, self.sem, self.base, self.n = eng, sem, base, 0

    def step(self, ins):
        self.n += 1
        ins.then_inc(self.sem, 1)

    def wait(self):
        wait(self.eng, self.sem, self.base + self.n)

    def __call__(self, ins):
        self.step(ins)
        self.wait()


def newton_rsqrt(v, n, x, y, t, scale):
    if n == 0:
        return v.tensor_scalar(t.bitcast(I32), x.bitcast(I32), 1, None, ALU.logical_shift_right)
    if n == 1:
        return v.tensor_scalar(y.bitcast(I32), t.bitcast(I32), -1.0, RSQRT_MAGIC, ALU.mult, ALU.add)
    if n == NEWTON_LINKS - 1:
        return v.tensor_scalar(y, y, scale, None, ALU.mult)
    if n % 3 == 2:
        return v.scalar_tensor_tensor(out=t, in0=y, scalar=-0.5, in1=y, op0=ALU.mult, op1=ALU.mult)
    if n % 3 == 0:
        return v.tensor_tensor(t, t, x, ALU.mult)
    return v.scalar_tensor_tensor(out=y, in0=t, scalar=1.5, in1=y, op0=ALU.add, op1=ALU.mult)


def layernorm_stats(dve, chain, rows, stats):
    for c, x in enumerate(rows):
        chain.step(dve.bn_stats(out=stats[:, c, :], in_=x))


def layernorm_combine(dve, chain, stats, mv, v, t):
    mean, half = mv[:, :, 0], mv[:, :, 1]
    chain.wait()
    chain.step(dve.scalar_tensor_tensor(out=v[:], in0=stats[:, :, 2], scalar=D * EPS, in1=stats[:, :, 5],
                                        op0=ALU.add, op1=ALU.add))
    chain.step(dve.tensor_tensor(mean, stats[:, :, 1], stats[:, :, 4], ALU.add))
    chain(dve.tensor_tensor(half, stats[:, :, 1], stats[:, :, 4], ALU.subtract))
    chain.step(dve.scalar_tensor_tensor(out=t[:], in0=half, scalar=0.25, in1=half, op0=ALU.mult, op1=ALU.mult))
    chain(dve.tensor_scalar(mean, mean, 0.5, None, ALU.mult))
    chain.step(dve.scalar_tensor_tensor(out=v[:], in0=v[:], scalar=1.0 / D, in1=t[:], op0=ALU.mult, op1=ALU.add))


def layernorm_apply(dve, chain, rows, mv, r, outs):
    for c, x in enumerate(rows):
        chain.step(dve.tensor_scalar(outs[c], x, mv[:, c, 0:1], r[:, c:c + 1], ALU.subtract, ALU.mult))


def setup(nc, sb, sem, args, T):
    ld, done = sem("const_loaded"), sem("split_done")
    loads = [sem(f"weights_loaded{i}") for i in range(5)]
    T["experts_loaded"] = sem("experts_loaded")
    part, ones = sem("hi_part_done"), sem("ones_done")
    with nc.Block() as block:
        @block.sync
        def _(sp):
            sp.dma_start(T["consts"][:], args["consts"]).then_inc(ld, 16)
            sp.dma_start(T["wall"][:], args["wall"]).then_inc(loads[0], 16)
            sp.dma_start(T["rw"][:], args["rw"]).then_inc(loads[1], 16)
            sp.dma_start(T["wo"][:], args["wo"]).then_inc(loads[2], 16)
            sp.dma_start(T["cos"][:], args["cos"]).then_inc(loads[3], 16)
            sp.dma_start(T["sin"][:], args["sin"]).then_inc(loads[4], 16)
            sp.wait_ge(ld, 16)
            for s in loads:
                sp.wait_ge(s, 16)
            sp.dma_start(T["experts"][:, 0:E * 2 * F], args["gu"]).then_inc(T["experts_loaded"], 16)
            sp.dma_start(T["experts"][:, E * 2 * F:], args["dp"]).then_inc(T["experts_loaded"], 16)

        @block.scalar
        def _(act):
            act.wait_ge(loads[0], 16)
            act.activation(T["wall_hi"][:], T["wall"][:], ACT.Copy).then_inc(part, 1)

        @block.gpsimd
        def _(pool):
            for n in range(2):
                pool.memset(T["v32"][n][:, :, :, HD:HA], 1.0).then_inc(ones, 1)
                pool.memset(T["v_hi"][n][:, :, :, HD:HA], 1.0).then_inc(ones, 1)
                pool.memset(T["v_lo"][n][:, :, :, HD:HA], 0.0).then_inc(ones, 1)
            pool.memset(T["minus_half"][:], -0.5).then_inc(ones, 1)
            pool.wait_ge(ones, 7)

        @block.vector
        def _(dve):
            for n in ("rw_hi", "rw_lo"):
                dve.memset(T[n][:].bitcast(F32), 0.0).then_inc(done, 1)
            dve.wait_ge(loads[1], 16)
            dve.wait_ge(done, 2)
            dve.tensor_copy(T["rw_hi"][:, 0:E], T["rw"][:]).then_inc(done, 1)
            dve.wait_ge(done, 3)
            dve.tensor_tensor(T["rw_lo"][:, 0:E], T["rw"][:], T["rw_hi"][:, 0:E].bitcast(F32),
                              ALU.subtract).then_inc(done, 1)
            dve.wait_ge(part, 1)
            dve.tensor_tensor(T["wall_lo"][:], T["wall"][:], T["wall_hi"][:].bitcast(F32),
                              ALU.subtract).then_inc(done, 1)
            dve.wait_ge(ld, 16)
            dve.tensor_copy(T["sel"][:], T["consts"][0:2 * E, C_SEL:]).then_inc(done, 1)
            dve.wait_ge(done, 6)


def attention(nc, st, sb, ps, sem, args, T):
    con = T["consts"]
    ident = con[:, C_ID:C_ID + P]
    tri = con[:, C_TRI:C_TRI + P].rearrange("p (o i) -> p o i", o=1).broadcast_to([P, 4, P])
    par_mask = [con[:, C_EVEN:C_EVEN + 1], con[:, C_ODD:C_ODD + 1]]

    xT = [sb(f"xT{i}", [P, 2 * P], F32) for i in range(2)]
    xT_hi = [sb(f"xT_hi{i}", [P, 2 * P], F32R) for i in range(2)]
    xT_lo = [sb(f"xT_lo{i}", [P, 2 * P], F32R) for i in range(2)]
    x_tok = [sb(f"x_tok{i}", [P, 4, D], F32) for i in range(2)]
    rot_a, rot_b = sb("rot_a", [P, 4 * D], F32), sb("rot_b", [P, 4 * D], F32)
    qk_tok = [sb(f"qk_tok{i}", [P, 2, 2 * D], F32) for i in range(2)]
    v32, v_hi, v_lo = T["v32"], T["v_hi"], T["v_lo"]
    gate = [sb(f"gate{i}", [P, 4, V], F32) for i in range(2)]
    q32 = [sb(f"q32_{i}", [P, 2, P], F32) for i in range(2)]
    q_hi = [sb(f"q_hi{i}", [P, 2, 2, P], F32R) for i in range(2)]
    q_lo = [sb(f"q_lo{i}", [P, 2, 2, P], F32R) for i in range(2)]
    k_hi = [sb(f"k_hi{i}", [P, 2, P], F32R) for i in range(2)]
    k_lo = [sb(f"k_lo{i}", [P, 2, P], F32R) for i in range(2)]
    s32 = [sb(f"s32_{g}", [P, 4 * P], F32) for g in range(4)]
    s_hi = [sb(f"s_hi{g}", [P, 4 * P], BF16) for g in range(4)]
    s_lo = [sb(f"s_lo{g}", [P, 4 * P], BF16) for g in range(4)]
    state = [sb(f"state{i}", [P, H * HA], F32) for i in range(2)]
    kv_masked = sb("kv_masked", [P, H * HA], F32)
    o_sb = [sb(f"o_sb{i}", [P, 4, H, HA], F32) for i in range(2)]
    o_sq = [sb(f"o_sq{i}", [P, H, HD], F32) for i in range(2)]
    o_ms = [sb(f"o_ms{i}", [P, 4, H], F32) for i in range(2)]
    rms_v, rms_t = sb("rms_v", [P, 4 * H], F32), sb("rms_t", [P, 4 * H], F32)
    rms_r = sb("rms_r", [P, 4 * H], F32)
    gated = sb("gated", [P, 4, V], F32)
    gT = sb("gT", [P, 4, 2, P], F32)
    resid = sb("resid", [P, 4, D], F32)
    ln_st, ln_mv = sb("ln_st", [P, 4, 6], F32), sb("ln_mv", [P, 4, 2], F32)
    ln_v, ln_t, ln_r = (sb(f"ln_{c}", [P, 4], F32) for c in "vtr")
    h1 = sb("h1", [P, 4, D], F32)
    lgT = sb("lgT", [P, GT], F32)

    ps_s = [ps(f"ps_s{g}", [P, 4 * P]) for g in range(4)]
    ps_o, ps_vg, ps_qk, ps_t = ps("ps_o", [P, 4 * P]), ps("ps_vg", [P, 4 * P]), ps("ps_qk", [P, 4 * P]), ps("ps_t", [P, 4 * P])

    xT_loaded = [sem(f"xT_loaded{i}") for i in range(2)]
    x_tok_loaded = [sem(f"x_tok_loaded{i}") for i in range(2)]
    xhi_done, xlo_done = sem("xhi_done"), sem("xlo_done")
    qk_proj, vg_proj = sem("qk_proj"), sem("vg_proj")
    rope_done, qktok_done, qkT_done = sem("rope_done"), sem("qktok_done"), sem("qkT_done")
    qkhi_done, qklo_done = sem("qkhi_done"), sem("qklo_done")
    v_done, vlo_done = sem("v_done"), sem("vlo_done")
    scores_done, s32_done = sem("scores_done"), sem("s32_done")
    shi_done, slo_done = sem("shi_done"), sem("slo_done")
    kv_done, kv_read, state_done = sem("kv_done"), sem("kv_read"), sem("state_done")
    o_done, osb_done, ms_done = sem("o_done"), sem("osb_done"), sem("ms_done")
    rms_chain, gate_done, gated_done = sem("rms_chain"), sem("gate_done"), sem("gated_done")
    gT_done, gT_read, wo_done = sem("gT_done"), sem("gT_read"), sem("wo_done")
    ln_chain, h1T_done = sem("ln_chain"), sem("h1T_done")
    h1hi_done, h1lo_done = sem("h1hi_done"), sem("h1lo_done")
    lgT_done, lgT_read, lg_done, lg_read = sem("lgT_done"), sem("lgT_read"), sem("lg_done"), sem("lg_read")
    ln_r_done = sem("ln_r_done")
    RMS_SUM = 3
    RMS_LINKS = RMS_SUM + NEWTON_LINKS
    LN_LINKS = 1 + LN_STATS + LN_COMBINE + LN_APPLY

    def steps(eng, body):
        for pp in range(-3, PAIRS):
            body(0, pp)
        for pp in range(PAIRS):
            body(1, pp)
        with eng.Fori(2, B - 1) as b:
            for pp in range(PAIRS):
                body(b, pp)
        for pp in range(PAIRS):
            body(B - 1, pp)
        for pp in range(PAIRS + 1):
            body(B, pp)

    def tail(b, pp):
        g = 2 * b + pp // 2
        if pp % 2 == 0:
            return g - 1, g - 2, g - 3
        return g - 1, g - 2

    def kv_before(b, pp):
        return (POS - 1) * b + min(2 * max(pp, 0), POS - 1)

    with nc.Block() as block:
        @block.sync
        def _(sp):
            def body(b, pp):
                n = PAIRS * b + pp
                if within(n + 3, NPAIR):
                    j = (pp + 1) % 2
                    wait(sp, xhi_done, n + 2)
                    wait(sp, xlo_done, n + 2)
                    sp.dma_start(xT[j][:], args["xT"][:, ds((n + 3) * 2 * P, 2 * P)]).then_inc(xT_loaded[j], 16)
                if within(n, NPAIR) and pp % 2 == 1:
                    g = 2 * b + pp // 2
                    wait(sp, ln_chain, LN_LINKS * (g - 2) + 1)
                    sp.dma_start(x_tok[pp // 2 % 2][:],
                                 args["x"][ds(g * GT, GT), :].rearrange("(c p) d -> p c d", p=P)
                                 ).then_inc(x_tok_loaded[pp // 2 % 2], 16)
            steps(sp, body)

        @block.tensor
        def _(pe):
            def three_pass(out, w_hi, w_lo, x_hi, x_lo, first=True, last=True):
                pe.matmul(out, w_hi, x_hi, start=first, stop=False)
                pe.matmul(out, w_hi, x_lo, start=False, stop=False)
                return pe.matmul(out, w_lo, x_hi, start=False, stop=last)

            def project_vg(n, i, c):
                x = slice(c * P, (c + 1) * P)
                three_pass(ps_vg[:], xT_hi[i][:, x], xT_lo[i][:, x], T["wall_hi"][:, 2 * D:],
                           T["wall_lo"][:, 2 * D:]).then_inc(vg_proj, 1)

            def tail_part(b, pp, part):
                if pp % 2 == 0:
                    g = tail(b, pp)[2]
                    if part == 0 and within(g, GROUPS):
                        pe.wait_ge(lgT_read, g + 1)
                        for c in range(4):
                            mm = pe.transpose(ps_t[:, c * P:(c + 1) * P], lgT[:, c * P:(c + 1) * P], ident)
                        mm.then_inc(lg_done, 1)
                    return
                g = tail(b, pp)[0]
                if not within(g, GROUPS):
                    return
                if part == 0:
                    pe.wait_ge(gated_done, g + 1)
                    wait(pe, h1hi_done, g)
                    wait(pe, h1lo_done, g)
                else:
                    pe.wait_ge(gT_read, 2 * g + 1)
                for k in range(4):
                    mm = pe.transpose(ps_t[:, k * P:(k + 1) * P],
                                      gated[:, 2 * part + k // 2, (k % 2) * P:(k % 2 + 1) * P], ident)
                mm.then_inc(gT_done, 1)

            def project_out(b, pp):
                g = tail(b, pp)[0]
                if within(g, GROUPS):
                    pe.wait_ge(gT_read, 2 * g + 2)
                    for c in range(4):
                        for k in range(2):
                            mm = pe.matmul(ps_t[:, c * P:(c + 1) * P], gT[:, c, k, :], T["wo"][:, k * D:(k + 1) * D],
                                           start=(k == 0), stop=(k == 1))
                    mm.then_inc(wo_done, 1)

            def body(b, pp):
                n = PAIRS * b + pp
                i, j = pp % 2, (pp + 1) % 2
                main, front = within(n, NPAIR), within(n + 1, NPAIR)
                ahead = within(n + 2, NPAIR)

                def update(c):
                    pos = 2 * pp + c
                    if pos < POS - 1:
                        wait(pe, kv_read, (POS - 1) * b + pos)
                        pe.matmul(ps_vg[:, 0:H * HA], qk_tok[i][:, c, D:2 * D],
                                  v32[i][:, c, :, :].rearrange("p h a -> p (h a)"),
                                  start=True, stop=True).then_inc(kv_done, 1)

                def values(c):
                    pos, m = 2 * pp + c, 2 * n + c
                    pe.wait_ge(vlo_done, m + 1)
                    wait(pe, osb_done, 2 * m)
                    for h in range(H):
                        if c == 0 and h % 2 == 0:
                            pe.wait_ge(shi_done, 4 * n + h // 2 + 1)
                            pe.wait_ge(slo_done, 4 * n + h // 2 + 1)
                        cols = slice((2 * c + h % 2) * P, (2 * c + h % 2 + 1) * P)
                        o = ps_o[:, h * HA:(h + 1) * HA]
                        for k, (s, v) in enumerate(((s_hi, v_hi), (s_hi, v_lo), (s_lo, v_hi))):
                            mm = pe.matmul(o, s[h // 2][:, cols], v[i][:, c, h, :], start=(h == 0 and k == 0),
                                           stop=(pos == 0), skip_group_check=True)
                    if pos:
                        if pos == 1:
                            pe.wait_ge(kv_read, (POS - 1) * b + 1)
                        else:
                            pe.wait_ge(state_done, (POS - 2) * b + pos - 1)
                        mm = pe.matmul(ps_o[:, 0:H * HA], q32[i][:, c, :], state[pos % 2][:],
                                       start=False, stop=True, skip_group_check=True)
                    mm.then_inc(o_done, 1)

                def first_vg():
                    if ahead:
                        wait(pe, v_done, 6 * (n + 2))
                        wait(pe, kv_read, kv_before(b, pp + 1))
                        project_vg(n + 2, i, 0)

                def second_vg():
                    if front:
                        pe.wait_ge(v_done, 6 * (n + 1) + 3)
                        project_vg(n + 1, j, 1)

                def scores(g):
                    wait(pe, s32_done, 4 * n + g + 1)
                    rows = slice(32 * g, 32 * g + 32)
                    for c in range(2):
                        mm = three_pass(ps_s[g][:, c * 2 * P:(c + 1) * 2 * P], k_hi[j][rows, c, :],
                                        k_lo[j][rows, c, :], q_hi[j][rows, c, :, :], q_lo[j][rows, c, :, :])
                    mm.then_inc(scores_done, 1)

                if front:
                    pe.wait_ge(qktok_done, n + 2)
                    for k in range(4):
                        mm = pe.transpose(ps_qk[:, k * P:(k + 1) * P],
                                          qk_tok[j][:, k % 2, (k // 2) * D:(k // 2 + 1) * D], ident)
                    mm.then_inc(qkT_done, 1)
                second_vg()
                if pp % 2 == 0:
                    _, summed, routed = tail(b, pp)
                    if within(routed, GROUPS):
                        pe.wait_ge(h1hi_done, routed + 1)
                        pe.wait_ge(h1lo_done, routed + 1)
                        if within(summed, GROUPS):
                            pe.wait_ge(ln_chain, LN_LINKS * summed + 1)
                        at = ds(routed * GT, GT)
                        three_pass(ps_t[:], T["rw_hi"][:], T["rw_lo"][:], T["h1T_hi"][:, at],
                                   T["h1T_lo"][:, at]).then_inc(lgT_done, 1)
                else:
                    g = tail(b, pp)[1]
                    if within(g, GROUPS):
                        pe.wait_ge(ln_chain, LN_LINKS * (g + 1))
                        wait(pe, lg_read, g)
                        for c in range(4):
                            mm = pe.transpose(ps_t[:, c * P:(c + 1) * P], h1[:, c, :], ident)
                        mm.then_inc(h1T_done, 1)
                if front and main:
                    pe.wait_ge(v_done, 6 * (n + 2))
                if main:
                    update(0)
                if front:
                    pe.wait_ge(qkhi_done, 4 * (n + 2))
                    pe.wait_ge(qklo_done, 3 * (n + 2))
                if ahead:
                    pe.wait_ge(xhi_done, n + 3)
                    pe.wait_ge(xlo_done, n + 3)
                    for c in range(2):
                        x = slice(c * P, (c + 1) * P)
                        mm = three_pass(ps_qk[:, c * 2 * D:(c + 1) * 2 * D], xT_hi[i][:, x], xT_lo[i][:, x],
                                        T["wall_hi"][:, 0:2 * D], T["wall_lo"][:, 0:2 * D])
                    mm.then_inc(qk_proj, 1)
                if main:
                    update(1)
                if front:
                    scores(0)
                    scores(1)
                if main:
                    values(0)
                tail_part(b, pp, 0)
                if front:
                    scores(2)
                    scores(3)
                if main:
                    values(1)
                if pp % 2 == 1:
                    tail_part(b, pp, 1)
                first_vg()
                if pp % 2 == 1:
                    project_out(b, pp)
            steps(pe, body)

        @block.scalar
        def _(act):
            def read_vg(b, pp, j, c):
                n = PAIRS * b + pp
                act.wait_ge(vg_proj, 2 * (n + 1) + c + 1)
                if c == 0:
                    wait(act, o_done, 2 * n)
                    wait(act, vlo_done, 2 * n)
                v = ps_vg[:, 0:V].rearrange("p (h d) -> p h d", d=HD)
                act.activation(v32[j][:, c, :, 0:HD], v, ACT.Copy).then_inc(v_done, 1)
                act.activation(v_hi[j][:, c, :, 0:HD], v, ACT.Copy).then_inc(v_done, 1)
                wait(act, gate_done, 2 * b + (pp + 1) // 2 - 1)
                act.activation(gate[(pp + 1) // 2 % 2][:, 2 * j + c, :], ps_vg[:, V:2 * V], ACT.Silu
                               ).then_inc(v_done, 1)

            def tail_part(b, pp, part):
                g = tail(b, pp)[2 if pp % 2 == 0 else 0]
                if not within(g, GROUPS):
                    return
                if pp % 2 == 1:
                    if part == 0:
                        wait(act, wo_done, g)
                    act.wait_ge(gT_done, 2 * g + part + 1)
                    act.activation(gT[:, 2 * part:2 * part + 2, :, :],
                                   ps_t[:].rearrange("p (c k i) -> p c k i", c=2, k=2), ACT.Copy
                                   ).then_inc(gT_read, 1)
                elif part == 0:
                    act.wait_ge(lg_done, g + 1)
                    act.activation(T["logits"][:, ds(g * 4 * E, 4 * E)].rearrange("p (c e) -> p c e", e=E),
                                   ps_t[:].rearrange("p (c e) -> p c e", e=P)[:, :, 0:E], ACT.Copy).then_inc(lg_read, 1)

            def body(b, pp):
                n = PAIRS * b + pp
                i, j = pp % 2, (pp + 1) % 2
                main, front = within(n, NPAIR), within(n + 1, NPAIR)
                q = ps_qk[:, 0:2 * P].rearrange("p (c i) -> p c i", c=2)
                k = ps_qk[:, 2 * P:].rearrange("p (c i) -> p c i", c=2)

                def upper_scores(g):
                    if main:
                        wait(act, o_done, 2 * n)
                        act.wait_ge(s32_done, 4 * n + g + 1)
                        act.activation(s_hi[g][:], s32[g][:], ACT.Copy).then_inc(shi_done, 1)

                upper_scores(0)
                if front:
                    read_vg(b, pp, j, 0)
                    act.wait_ge(qkT_done, n + 2)
                    for par in range(2):
                        act.activation(q_hi[j][:, :, par, :], q, ACT.Copy, scale=par_mask[par]).then_inc(qkhi_done, 1)
                    act.activation(k_hi[j][:], k, ACT.Copy).then_inc(qkhi_done, 1)
                upper_scores(1)
                if front:
                    act.activation(q32[j][:], q, ACT.Copy).then_inc(qkhi_done, 1)
                    read_vg(b, pp, j, 1)
                upper_scores(2)
                upper_scores(3)
                g = tail(b, pp)[2 if pp % 2 == 0 else 1]
                if pp % 2 == 0 and within(g, GROUPS):
                    act.wait_ge(lgT_done, g + 1)
                    wait(act, lg_done, g)
                    act.activation(lgT[:], ps_t[:], ACT.Copy).then_inc(lgT_read, 1)
                if pp % 2 == 1 and within(g, GROUPS):
                    act.wait_ge(h1T_done, g + 1)
                    act.activation(T["h1T_hi"][:, ds(g * GT, GT)], ps_t[:], ACT.Copy).then_inc(h1hi_done, 1)
                if within(n + 3, NPAIR):
                    act.wait_ge(xT_loaded[j], 16 * (2 * b + (pp + 3) // 2 + 1))
                    wait(act, vg_proj, 2 * (n + 2))
                    wait(act, xlo_done, n + 2)
                    act.activation(xT_hi[j][:], xT[j][:], ACT.Copy).then_inc(xhi_done, 1)
                if main:
                    if pp % 2 == 0:
                        wait(act, gated_done, 2 * b + pp // 2 - 1)
                    for c in range(2):
                        m = 2 * n + c
                        act.wait_ge(o_done, m + 1)
                        o = ps_o[:, 0:H * HA].rearrange("p (h a) -> p h a", a=HA)
                        act.activation(o_sb[pp // 2 % 2][:, 2 * i + c, :, :], o, ACT.Copy).then_inc(osb_done, 1)
                        wait(act, ms_done, m - 1)
                        act.activation(o_sq[c][:], o[:, :, 0:HD], ACT.Square).then_inc(osb_done, 1)
                        tail_part(b, pp, c)
                if not main:
                    tail_part(b, pp, 0)
                    tail_part(b, pp, 1)
            steps(act, body)

        @block.gpsimd
        def _(pool):
            def v_lower(n, j, c):
                pool.wait_ge(v_done, 6 * (n + 1) + 3 * c + 2)
                pool.tensor_tensor(v_lo[j][:, c, :, 0:HD], v32[j][:, c, :, 0:HD], v_hi[j][:, c, :, 0:HD],
                                   ALU.subtract).then_inc(vlo_done, 1)

            def body(b, pp):
                n = PAIRS * b + pp
                i, j = pp % 2, (pp + 1) % 2
                main, front = within(n, NPAIR), within(n + 1, NPAIR)
                if main:
                    wait(pool, o_done, 2 * n)
                    for g in range(4):
                        pool.wait_ge(shi_done, 4 * n + g + 1)
                        pool.tensor_tensor(s_lo[g][:], s32[g][:], s_hi[g][:], ALU.subtract).then_inc(slo_done, 1)
                if front:
                    v_lower(n, j, 0)
                    v_lower(n, j, 1)
                if pp % 2 == 0:
                    summed = tail(b, pp)[1]
                    if within(summed, GROUPS):
                        pool.wait_ge(ln_chain, LN_LINKS * (summed + 1) - LN_APPLY)
                        pool.tensor_tensor(ln_r[:], ln_v[:], T["minus_half"][:], ALU.pow).then_inc(ln_r_done, 1)
                if within(n + 2, NPAIR):
                    pool.wait_ge(rope_done, 2 * (n + 3))
                    wait(pool, kv_done, kv_before(b, pp + 1))
                    pool.tensor_tensor(qk_tok[i][:].rearrange("p c d -> p (c d)"), rot_a[:], rot_b[:], ALU.add
                                       ).then_inc(qktok_done, 1)
                if pp % 2 == 0:
                    g = tail(b, pp)[0]
                    if within(g, GROUPS):
                        pool.wait_ge(rms_chain, RMS_LINKS * (g + 1))
                        pool.wait_ge(v_done, 6 * 2 * (g + 1))
                        wait(pool, gT_done, 2 * g)
                        r = rms_r[:].rearrange("p (h o) -> p h o", o=1).broadcast_to([P, 4 * H, HD])
                        by_head = "p c (h d) -> p (c h) d"
                        pool.tensor_tensor(gated[:].rearrange(by_head, d=HD),
                                           gate[(pp // 2 - 1) % 2][:].rearrange(by_head, d=HD), r, ALU.mult
                                           ).then_inc(gate_done, 1)
                if within(n + 3, NPAIR):
                    pool.wait_ge(xhi_done, n + 4)
                    pool.tensor_tensor(xT_lo[j][:], xT[j][:], xT_hi[j][:].bitcast(F32), ALU.subtract
                                       ).then_inc(xlo_done, 1)
            steps(pool, body)

        @block.vector
        def _(dve):
            def body(b, pp):
                n = PAIRS * b + pp
                i, j = pp % 2, (pp + 1) % 2
                main, front = within(n, NPAIR), within(n + 1, NPAIR)
                even = pp % 2 == 0
                rooted, summed = (tail(b, pp)[0], tail(b, pp)[1]) if even else (-1, -1)
                gating, applied = (-1, -1) if even else tail(b, pp)
                newton = Chain(dve, rms_chain, RMS_LINKS * rooted + RMS_SUM)

                def newton_link():
                    if not within(rooted, GROUPS) or newton.n == NEWTON_LINKS:
                        return
                    if newton.n == 1:
                        wait(dve, gate_done, rooted)
                    newton.wait()
                    newton.step(newton_rsqrt(dve, newton.n, rms_v[:], rms_r[:], rms_t[:], float(HD) ** 0.5))

                newton_link()
                rows = [resid[:, c, :] for c in range(4)]
                def product_read(c):
                    pos, m = 2 * pp + c, 2 * n + c
                    newton_link()
                    if pos < POS - 1:
                        dve.wait_ge(kv_done, (POS - 1) * b + pos + 1)
                        if pos == 0:
                            wait(dve, o_done, m)
                        wait(dve, state_done, (POS - 2) * b + max(pos - 1, 0))
                        out = state[1] if pos == 0 else kv_masked
                        dve.tensor_tensor(out[:], ps_vg[:, 0:H * HA], con[:, C_DECAY:C_GAMMA], ALU.mult
                                          ).then_inc(kv_read, 1)

                def state_update(c):
                    pos, m = 2 * pp + c, 2 * n + c
                    newton_link()
                    if 0 < pos < POS - 1:
                        dve.wait_ge(kv_read, (POS - 1) * b + pos + 1)
                        wait(dve, o_done, m)
                        dve.scalar_tensor_tensor(out=state[(pos + 1) % 2][:], in0=state[pos % 2][:],
                                                 scalar=con[:, C_GAMMA:C_GAMMA + 1], in1=kv_masked[:],
                                                 op0=ALU.mult, op1=ALU.add).then_inc(state_done, 1)

                def causal(g):
                    if front:
                        newton_link()
                        dve.wait_ge(scores_done, 4 * (n + 1) + g + 1)
                        wait(dve, slo_done, 4 * n + g + 1)
                        dve.tensor_tensor(s32[g][:].rearrange("p (r i) -> p r i", i=P),
                                          ps_s[g][:].rearrange("p (r i) -> p r i", i=P), tri, ALU.mult
                                          ).then_inc(s32_done, 1)

                if within(summed, GROUPS):
                    ln = Chain(dve, ln_chain, LN_LINKS * summed)
                    ln.wait()
                    dve.wait_ge(wo_done, summed + 1)
                    dve.wait_ge(x_tok_loaded[pp // 2 % 2], 16 * (b + pp // 2 // 2))
                    ln.step(dve.tensor_tensor(resid[:].rearrange("p c d -> p (c d)"), ps_t[:],
                                              x_tok[pp // 2 % 2][:].rearrange("p c d -> p (c d)"), ALU.add))
                    newton_link()
                    ln.wait()
                    layernorm_stats(dve, ln, rows, ln_st)
                if within(applied, GROUPS):
                    ln = Chain(dve, ln_chain, LN_LINKS * (applied + 1) - LN_APPLY)
                    ln.wait()
                    dve.wait_ge(ln_r_done, applied + 1)
                    wait(dve, h1T_done, applied)
                    layernorm_apply(dve, ln, rows, ln_mv, ln_r, [h1[:, c, :] for c in range(4)])
                if within(gating, GROUPS):
                    dve.wait_ge(gate_done, gating + 1)
                    gv = gated[:].rearrange("p c (h d) -> p c h d", d=HD)
                    dve.tensor_tensor(gv, o_sb[(pp // 2 - 1) % 2][:, :, :, 0:HD], gv, ALU.mult
                                      ).then_inc(gated_done, 1)
                newton_link()
                if front:
                    dve.wait_ge(qkhi_done, 4 * (n + 2))
                    q = ps_qk[:, 0:2 * P].rearrange("p (c i) -> p c i", c=2)
                    k = ps_qk[:, 2 * P:].rearrange("p (c i) -> p c i", c=2)
                    for par in range(2):
                        dve.scalar_tensor_tensor(out=q_lo[j][:, :, par, :], in0=q, scalar=par_mask[par],
                                                 in1=q_hi[j][:, :, par, :].bitcast(F32), op0=ALU.mult,
                                                 op1=ALU.subtract).then_inc(qklo_done, 1)
                        newton_link()
                    dve.tensor_tensor(k_lo[j][:], k, k_hi[j][:].bitcast(F32), ALU.subtract).then_inc(qklo_done, 1)
                if within(summed, GROUPS):
                    wait(dve, ln_r_done, summed)
                    layernorm_combine(dve, Chain(dve, ln_chain, LN_LINKS * summed + 1 + LN_STATS), ln_st, ln_mv,
                                      ln_v, ln_t)
                if main:
                    product_read(0)
                    state_update(0)
                if within(n + 2, NPAIR):
                    dve.wait_ge(qk_proj, n + 3)
                    wait(dve, qktok_done, n + 2)
                    at = slice((pp + 2) % PAIRS * 4 * D, ((pp + 2) % PAIRS + 1) * 4 * D)
                    two = "p (d t) -> p d t"
                    dve.tensor_tensor(rot_a[:], ps_qk[:], T["cos"][:, at], ALU.mult).then_inc(rope_done, 1)
                    newton_link()
                    dve.tensor_tensor(rot_b[:].rearrange(two, t=2), ps_qk[:].rearrange(two, t=2)[:, :, ::-1],
                                      T["sin"][:, at].rearrange(two, t=2), ALU.mult).then_inc(rope_done, 1)
                if within(applied, GROUPS):
                    dve.wait_ge(h1hi_done, applied + 1)
                    at = ds(applied * GT, GT)
                    dve.tensor_tensor(T["h1T_lo"][:, at], ps_t[:], T["h1T_hi"][:, at].bitcast(F32), ALU.subtract
                                      ).then_inc(h1lo_done, 1)
                causal(0)
                causal(1)
                if main:
                    product_read(1)
                causal(2)
                causal(3)
                if main:
                    state_update(1)
                    for c in range(2):
                        newton_link()
                        dve.wait_ge(osb_done, 2 * (2 * n + c + 1))
                        dve.tensor_reduce(o_ms[pp // 2 % 2][:, 2 * i + c, :], o_sq[c][:], AX_X, ALU.add
                                          ).then_inc(ms_done, 1)
                if within(rooted, GROUPS):
                    while newton.n < NEWTON_LINKS:
                        newton_link()
                if main and not even:
                    g = 2 * b + pp // 2
                    link = Chain(dve, rms_chain, RMS_LINKS * g)
                    link.wait()
                    dve.wait_ge(ms_done, 4 * (g + 1))
                    v = rms_v[:].rearrange("p (c h) -> p c h", h=H)
                    total = o_sb[pp // 2 % 2][:, :, :, HD]
                    guard = con[:, C_GUARD + pp // 2 * 4 * H:C_GUARD + (pp // 2 + 1) * 4 * H]
                    link(dve.scalar_tensor_tensor(out=v, in0=total, scalar=HD * EPS, in1=total,
                                                  op0=ALU.mult, op1=ALU.mult))
                    link(dve.tensor_tensor(rms_v[:], rms_v[:], guard, ALU.max))
                    link.step(dve.tensor_tensor(v, v, o_ms[pp // 2 % 2][:], ALU.add))
            steps(dve, body)


def routing(nc, sb, ps, sem, T):
    W = NCH * E
    lg = T["logits"]
    con = T["consts"]
    by = "p (n e) -> p n e"
    hot1, hot2, tmp, left = (sb(n, [P, W], F32) for n in ("hot1", "hot2", "tmp", "left"))
    top1, top2, at, gap, ratio, den, w1, w2 = (sb(n, [P, NCH], F32) for n in (
        "top1", "top2", "at", "gap", "ratio", "den", "w1", "w2"))
    wts = sb("wts", [P, W], F32)
    parts = sb("parts", [P, NCH, 2 * E], F32R)
    banks = [ps(f"ps_w{n}", [2 * E, GT]) for n in range(8)]
    chain, exp_done, parts_done = sem("routing_chain"), sem("exp_done"), sem("parts_done")
    tr_done, read_even, read_odd = sem("weights_transposed"), sem("read_even"), sem("read_odd")
    ehi, elo = sem("experts_hi_done"), sem("experts_lo_done")
    idx = con[:, C_IDX:C_IDX + E].rearrange("p (o e) -> p o e", o=1).broadcast_to([P, NCH, E])

    def each(col):
        return col[:].rearrange("p (n o) -> p n o", o=1).broadcast_to([P, NCH, E])

    def table(t):
        return t[:].rearrange(by, e=E)

    QUARTER = E * 3 * F // 4
    with nc.Block() as block:
        @block.vector
        def _(dve):
            link = Chain(dve, chain, 0)
            scores = lg
            for top, hot in ((top1, hot1), (top2, hot2)):
                link(dve.tensor_reduce(top[:], table(scores), AX_X, ALU.max))
                link(dve.tensor_tensor(table(tmp), table(scores), each(top), ALU.is_equal))
                link(dve.tensor_tensor(table(tmp), table(tmp), idx, ALU.mult))
                link(dve.tensor_reduce(at[:], table(tmp), AX_X, ALU.max))
                link(dve.tensor_tensor(table(hot), idx, each(at), ALU.is_equal))
                if top is top1:
                    link(dve.scalar_tensor_tensor(out=left[:], in0=hot[:], scalar=-3.0e38, in1=lg[:],
                                                  op0=ALU.mult, op1=ALU.add))
                    scores = left
            link(dve.tensor_tensor(gap[:], top2[:], top1[:], ALU.subtract))
            dve.wait_ge(exp_done, 1)
            link(dve.tensor_scalar(den[:], ratio[:], 1.0, None, ALU.add))
            link(dve.reciprocal(w1[:], den[:]))
            link(dve.tensor_tensor(w2[:], ratio[:], w1[:], ALU.mult))
            link(dve.tensor_tensor(table(hot1), table(hot1), each(w1), ALU.mult))
            link(dve.tensor_tensor(table(hot2), table(hot2), each(w2), ALU.mult))
            link(dve.tensor_tensor(wts[:], hot1[:], hot2[:], ALU.add))
            link(dve.tensor_copy(parts[:, :, 0:E], table(wts)))
            dve.tensor_tensor(parts[:, :, E:2 * E], table(wts), parts[:, :, 0:E].bitcast(F32), ALU.subtract
                              ).then_inc(parts_done, 1)
            for g in range(1, GROUPS, 2):
                dve.wait_ge(tr_done, g + 1)
                dve.tensor_copy(T["wT"][:, g * GT:(g + 1) * GT], banks[g % 8][:]).then_inc(read_odd, 1)
            dve.wait_ge(read_odd, GROUPS // 2)

        @block.scalar
        def _(act):
            act.wait_ge(T["experts_loaded"], 32)
            for n in range(4):
                part = slice(n * QUARTER, (n + 1) * QUARTER)
                act.activation(T["experts_hi"][:, part], T["experts"][:, part], ACT.Copy).then_inc(ehi, 1)
            act.wait_ge(chain, 12)
            act.activation(ratio[:], gap[:], ACT.Exp).then_inc(exp_done, 1)
            for g in range(0, GROUPS, 2):
                act.wait_ge(tr_done, g + 1)
                act.activation(T["wT"][:, g * GT:(g + 1) * GT], banks[g % 8][:], ACT.Copy).then_inc(read_even, 1)
            act.wait_ge(read_even, GROUPS // 2)

        @block.gpsimd
        def _(pool):
            for n in range(4):
                part = slice(n * QUARTER, (n + 1) * QUARTER)
                pool.wait_ge(ehi, n + 1)
                pool.tensor_tensor(T["experts_lo"][:, part], T["experts"][:, part],
                                   T["experts_hi"][:, part].bitcast(F32), ALU.subtract).then_inc(elo, 1)
            pool.wait_ge(elo, 4)

        @block.tensor
        def _(pe):
            pe.wait_ge(parts_done, 1)
            for g in range(GROUPS):
                wait(pe, read_odd if g % 2 else read_even, (g - 8) // 2 + 1)
                for c in range(4):
                    mm = pe.transpose(banks[g % 8][:, c * P:(c + 1) * P], parts[:, 4 * g + c, :].bitcast(F32),
                                      con[:, C_ID:C_ID + P])
                mm.then_inc(tr_done, 1)


def experts(nc, sb, ps, sem, args, T):
    con = T["consts"]
    ident = con[:, C_ID:C_ID + P]
    act_s = [sb(f"act_s{i}", [P, GT], F32) for i in range(2)]
    w_sb = [sb(f"w_sb{i}", [P, GT], F32) for i in range(2)]
    uw = sb("uw", [P, GT], F32)
    a32 = [sb(f"a32_{i}", [P, GT], F32) for i in range(2)]
    a_hi = [sb(f"a_hi{i}", [P, GT], F32R) for i in range(2)]
    a_lo = [sb(f"a_lo{i}", [P, GT], F32R) for i in range(2)]
    z1, z = sb("z1", [P, GT], F32), sb("z", [P, GT], F32)
    z_tok = sb("z_tok", [P, GT], F32)
    ln_st, ln_mv = sb("ln2_st", [P, 4, 6], F32), sb("ln2_mv", [P, 4, 2], F32)
    ln_v, ln_t, ln_r = (sb(f"ln2_{c}", [P, 4], F32) for c in "vtr")
    y = [sb(f"y{i}", [P, 4, D], F32) for i in range(2)]
    ps_gate = [ps(f"ps_gate{i}", [P, GT]) for i in range(2)]
    ps_up = [ps(f"ps_up{i}", [P, GT]) for i in range(2)]
    ps_w = [ps(f"ps_wt{i}", [P, GT]) for i in range(2)]
    ps_acc = [ps(f"ps_acc{i}", [P, GT]) for i in range(2)]

    gate_mm, w_mm, up_mm = sem("gate_mm"), sem("w_mm"), sem("up_mm")
    silu_done, wsb_done, uw_done, a_done = sem("silu_done"), sem("wsb_done"), sem("uw_done"), sem("a_done")
    ahi_done, alo_done, down_mm = sem("ahi_done"), sem("alo_done"), sem("down_mm")
    z1_done, z_done, zT_done, ztok_done = sem("z1_done"), sem("z_done"), sem("zT_done"), sem("ztok_done")
    ln_chain, ln_r_done = sem("ln2_chain"), sem("ln2_r_done")
    stored = [sem(f"stored{i}") for i in range(2)]
    LN_LINKS = LN_STATS + LN_COMBINE + LN_APPLY
    ROUND = 2 * E
    TURNS = GROUPS // 2
    STEPS = GROUPS * E

    def steps(eng, body, ahead):
        for k in range(-ahead, ROUND):
            body(0, k)
        with eng.Fori(1, TURNS - 1) as t:
            for k in range(ROUND):
                body(t, k)
        for k in range(ROUND):
            body(TURNS - 1, k)
        for k in range(6):
            body(TURNS, k)

    with nc.Block() as block:
        @block.tensor
        def _(pe):
            def three_pass(out, w_hi, w_lo, x_hi, x_lo, first=True, last=True):
                pe.matmul(out, w_hi, x_hi, start=first, stop=False)
                pe.matmul(out, w_lo, x_hi, start=False, stop=False)
                return pe.matmul(out, w_hi, x_lo, start=False, stop=last)

            def body(t, k):
                n = ROUND * t + k
                if within(n + 2, STEPS):
                    e, i = (k + 2) % E, k % 2
                    at = ds((2 * t + (k + 2) // E) * GT, GT)
                    hi, lo = T["experts_hi"], T["experts_lo"]
                    xh, xl = T["h1T_hi"][:, at], T["h1T_lo"][:, at]
                    g = slice(e * 2 * F, e * 2 * F + F)
                    u = slice(e * 2 * F + F, (e + 1) * 2 * F)
                    wait(pe, silu_done, n + 1)
                    wait(pe, wsb_done, n + 1)
                    three_pass(ps_gate[i][:], hi[:, g], lo[:, g], xh, xl).then_inc(gate_mm, 1)
                    pe.matmul(ps_w[i][:], T["sel"][:, e * P:(e + 1) * P], T["wT"][:, at], start=True, stop=True
                              ).then_inc(w_mm, 1)
                    wait(pe, uw_done, n + 1)
                    three_pass(ps_up[i][:], hi[:, u], lo[:, u], xh, xl).then_inc(up_mm, 1)
                if within(n - 1, STEPS):
                    e, i = (k - 1) % E, (k - 1) % 2
                    w = slice(E * 2 * F + e * D, E * 2 * F + (e + 1) * D)
                    pe.wait_ge(alo_done, n)
                    pe.matmul(ps_acc[(k - 1) // E % 2][:], T["experts_hi"][:, w], a_lo[i][:], start=False,
                              stop=(e == E - 1)).then_inc(down_mm, 1)
                if within(n, STEPS):
                    e, i = k % E, k % 2
                    w = slice(E * 2 * F + e * D, E * 2 * F + (e + 1) * D)
                    acc = ps_acc[k // E % 2][:]
                    pe.wait_ge(ahi_done, n + 1)
                    if e == 0:
                        wait(pe, ztok_done, 2 * t + k // E - 1)
                    hi, lo = T["experts_hi"], T["experts_lo"]
                    pe.matmul(acc, hi[:, w], a_hi[i][:], start=(e == 0), stop=False)
                    pe.matmul(acc, lo[:, w], a_hi[i][:], start=False, stop=False)
                done = 2 * t + k // E - 1
                if k % E == 2 and within(done, GROUPS):
                    pe.wait_ge(z_done, done + 1)
                    bank = ps_acc[(k // E - 1) % 2]
                    for c in range(4):
                        mm = pe.transpose(bank[:, c * P:(c + 1) * P], z[:, c * P:(c + 1) * P], ident)
                    mm.then_inc(zT_done, 1)
            steps(pe, body, 2)

        @block.scalar
        def _(act):
            def body(t, k):
                n = ROUND * t + k
                if within(n + 1, STEPS):
                    i = (k + 1) % 2
                    act.wait_ge(gate_mm, n + 2)
                    wait(act, a_done, n)
                    act.activation(act_s[i][:], ps_gate[i][:], ACT.Silu).then_inc(silu_done, 1)
                    act.wait_ge(w_mm, n + 2)
                    wait(act, uw_done, n)
                    act.activation(w_sb[i][:], ps_w[i][:], ACT.Copy).then_inc(wsb_done, 1)
                if within(n, STEPS):
                    i = k % 2
                    act.wait_ge(a_done, n + 1)
                    wait(act, down_mm, n - 1)
                    act.activation(a_hi[i][:], a32[i][:], ACT.Copy).then_inc(ahi_done, 1)
                done = 2 * t + k // E - 1
                if k % E == 2 and within(done, GROUPS):
                    act.wait_ge(zT_done, done + 1)
                    wait(act, ln_chain, LN_LINKS * done)
                    act.activation(z_tok[:], ps_acc[(k // E - 1) % 2][:], ACT.Copy).then_inc(ztok_done, 1)
            steps(act, body, 1)

        @block.gpsimd
        def _(pool):
            def body(t, k):
                n = ROUND * t + k
                if within(n, STEPS):
                    i = k % 2
                    pool.wait_ge(ahi_done, n + 1)
                    wait(pool, down_mm, n - 1)
                    pool.tensor_tensor(a_lo[i][:], a32[i][:], a_hi[i][:].bitcast(F32), ALU.subtract
                                       ).then_inc(alo_done, 1)
                done = 2 * t + k // E - 1
                if k % E == 4 and within(done, GROUPS):
                    pool.wait_ge(ln_chain, LN_LINKS * done + LN_STATS + LN_COMBINE)
                    pool.tensor_tensor(ln_r[:], ln_v[:], T["minus_half"][:], ALU.pow).then_inc(ln_r_done, 1)
            steps(pool, body, 0)

        @block.vector
        def _(dve):
            def body(t, k):
                n = ROUND * t + k
                if within(n, STEPS):
                    i = k % 2
                    dve.wait_ge(wsb_done, n + 1)
                    dve.wait_ge(up_mm, n + 1)
                    wait(dve, a_done, n)
                    dve.tensor_tensor(uw[:], w_sb[i][:], ps_up[i][:], ALU.mult).then_inc(uw_done, 1)
                    dve.wait_ge(uw_done, n + 1)
                    dve.wait_ge(silu_done, n + 1)
                    wait(dve, alo_done, n - 1)
                    dve.tensor_tensor(a32[i][:], act_s[i][:], uw[:], ALU.mult).then_inc(a_done, 1)
                done, i = 2 * t + k // E - 1, (k // E - 1) % 2
                if k % E == 1 and within(done, GROUPS):
                    at = ds(done * GT, GT)
                    dve.wait_ge(down_mm, E * (done + 1))
                    wait(dve, z_done, done)
                    dve.tensor_tensor(z1[:], ps_acc[i][:], T["h1T_hi"][:, at].bitcast(F32), ALU.add
                                      ).then_inc(z1_done, 1)
                    dve.wait_ge(z1_done, done + 1)
                    wait(dve, zT_done, done)
                    dve.tensor_tensor(z[:], z1[:], T["h1T_lo"][:, at].bitcast(F32), ALU.add).then_inc(z_done, 1)
                rows = [z_tok[:, c * P:(c + 1) * P] for c in range(4)]
                if k % E == 3 and within(done, GROUPS):
                    dve.wait_ge(ztok_done, done + 1)
                    layernorm_stats(dve, Chain(dve, ln_chain, LN_LINKS * done), rows, ln_st)
                if k % E == 4 and within(done, GROUPS):
                    wait(dve, ln_r_done, done)
                    layernorm_combine(dve, Chain(dve, ln_chain, LN_LINKS * done + LN_STATS), ln_st, ln_mv,
                                      ln_v, ln_t)
                if k % E == 5 and within(done, GROUPS):
                    dve.wait_ge(ln_chain, LN_LINKS * done + LN_STATS + LN_COMBINE)
                    dve.wait_ge(ln_r_done, done + 1)
                    wait(dve, stored[i], 16 * (t + (k // E - 1) // 2))
                    layernorm_apply(dve, Chain(dve, ln_chain, LN_LINKS * done + LN_STATS + LN_COMBINE), rows,
                                    ln_mv, ln_r, [y[i][:, c, :] for c in range(4)])
            steps(dve, body, 0)

        @block.sync
        def _(sp):
            def store(g, i):
                sp.wait_ge(ln_chain, LN_LINKS * (g + 1))
                sp.dma_start(args["out"][ds(g * GT, GT), :].rearrange("(c p) d -> p c d", p=P), y[i][:]
                             ).then_inc(stored[i], 16)
            with sp.Fori(0, TURNS) as t:
                for i in range(2):
                    store(2 * t + i, i)
            for i in range(2):
                sp.wait_ge(stored[i], 16 * TURNS)


def build(nc, args):
    T = {}
    with ExitStack() as keep:
        def pool_of(stack):
            def sb(name, shape, dt):
                return stack.enter_context(nc.sbuf_tensor(name, shape, dt))

            def ps(name, shape):
                return stack.enter_context(nc.psum_tensor(name, shape, F32))
            return sb, ps

        def sem(name):
            return keep.enter_context(nc.semaphore(name))

        sb, _ = pool_of(keep)
        T["consts"] = sb("consts", [P, C_END], F32)
        T["sel"] = sb("sel", [2 * E, E * P], F32R)
        T["experts"] = sb("experts", [P, E * 3 * F], F32)
        T["h1T_hi"] = sb("h1T_hi", [P, B * S], F32R)
        T["h1T_lo"] = sb("h1T_lo", [P, B * S], F32R)
        T["minus_half"] = sb("minus_half", [P, 4], F32)
        T["logits"] = sb("logits", [P, NCH * E], F32)
        with ExitStack() as own:
            sb, ps = pool_of(own)
            for n, w in (("wo", 2 * D), ("cos", POS * 2 * D), ("sin", POS * 2 * D)):
                T[n] = sb(n, [P, w], F32)
            T["wall_hi"], T["wall_lo"] = (sb(n, [P, 2 * D + 2 * V], F32R) for n in ("wall_hi", "wall_lo"))
            T["rw_hi"], T["rw_lo"] = (sb(n, [P, P], F32R) for n in ("rw_hi", "rw_lo"))
            for n, dt in (("v32", F32), ("v_hi", BF16), ("v_lo", BF16)):
                T[n] = [sb(f"{n}_{i}", [P, 2, H, HA], dt) for i in range(2)]
            with ExitStack() as staging:
                T["wall"] = pool_of(staging)[0]("wall", [P, 2 * D + 2 * V], F32)
                T["rw"] = pool_of(staging)[0]("rw", [P, E], F32)
                setup(nc, sb, sem, args, T)
            attention(nc, own, sb, ps, sem, args, T)
        T["wT"] = pool_of(keep)[0]("wT", [2 * E, B * S], F32R)
        T["experts_hi"] = pool_of(keep)[0]("experts_hi", [P, E * 3 * F], F32R)
        T["experts_lo"] = pool_of(keep)[0]("experts_lo", [P, E * 3 * F], F32R)
        with ExitStack() as own:
            routing(nc, *pool_of(own), sem, T)
        with ExitStack() as own:
            experts(nc, *pool_of(own), sem, args, T)


def kernel(**inputs):
    import concourse.bacc as bacc
    from concourse.bass_utils import run_bass_kernel_spmd

    consts, cos, sin = shape_constants()
    a = {k: np.asarray(v) for k, v in inputs.items()}
    x = a["L0_attn_x"].reshape(B * S, D)
    arrays = {
        "x": np.ascontiguousarray(x),
        "xT": np.ascontiguousarray(x.T),
        "wall": np.ascontiguousarray(np.concatenate([a["L0_attn_" + n] for n in ("wq", "wk", "wv", "wg")], axis=1)),
        "wo": np.ascontiguousarray(a["L0_attn_wo"].reshape(2, P, D).transpose(1, 0, 2).reshape(P, 2 * D)),
        "rw": np.ascontiguousarray(a["L0_ffn_router_weight"].T),
        "gu": np.ascontiguousarray(a["L0_ffn_gate_up_proj"].transpose(2, 0, 1).reshape(D, E * 2 * F)),
        "dp": np.ascontiguousarray(a["L0_ffn_down_proj"].transpose(2, 0, 1).reshape(F, E * D)),
        "consts": consts, "cos": cos, "sin": sin,
    }
    nc = bacc.Bacc("TRN2", target_bir_lowering=False, num_devices=1)
    args = {n: nc.dram_tensor(f"in_{n}", v.shape, mybir.dt.from_np(v.dtype), kind="ExternalInput").ap()
            for n, v in arrays.items()}
    args["out"] = nc.dram_tensor("out_y", (B * S, D), F32, kind="ExternalOutput").ap()
    build(nc, args)
    r = run_bass_kernel_spmd(nc, [{f"in_{n}": v for n, v in arrays.items()}], core_ids=[0])
    return r.results[0]["out_y"].reshape(B, S, D)
```

```python
from contextlib import ExitStack

import numpy as np
import concourse.bass as bass
from concourse import mybir

F32 = mybir.dt.float32
F32R = mybir.dt.float32r
BF16 = mybir.dt.bfloat16
I32 = mybir.dt.int32
ALU = mybir.AluOpType
ACT = mybir.ActivationFunctionType
AX_X = mybir.AxisListType.X
ds = bass.ds

B, S, D = 8, 1024, 128
H, KD, HD = 8, 16, 32
V = H * HD
HA = HD + 1
E, F = 8, 128
P = 128
POS = S // P
PAIRS = POS // 2
NPAIR = B * PAIRS
GROUPS = NPAIR // 2
GT = 4 * P
NCH = B * POS
EPS = 1e-5
RSQRT_MAGIC = float(0x5F3759DF)
NEWTON_LINKS = 2 + 3 * 3 + 1
LN_STATS, LN_COMBINE = 4, 6

C_ID, C_TRI, C_DECAY = 0, 128, 256
C_GAMMA = C_DECAY + H * HA
C_EVEN, C_ODD = C_GAMMA + 1, C_GAMMA + 2
C_GUARD = C_ODD + 1
C_IDX = C_GUARD + POS * H
C_END = C_IDX + E


def shape_constants():
    c = np.zeros((P, C_END), np.float32)
    t = np.arange(P)
    decay = np.log1p(-2.0 ** (-5.0 - np.arange(H)))
    c[:, C_ID:C_ID + P] = np.eye(P)
    c[:, C_TRI:C_TRI + P] = t[:, None] <= t[None, :]
    head = t // KD
    block = (head[:, None] == np.arange(H)[None, :]) * np.exp(P * decay)[None, :]
    c[:, C_DECAY:C_GAMMA] = np.repeat(block, HA, axis=1)
    c[:, C_GAMMA] = np.exp(P * decay)[head]
    c[:, C_EVEN] = head % 2 == 0
    c[:, C_ODD] = head % 2 == 1
    i = np.arange(S)
    total = (1 - np.exp((i[:, None] + 1) * decay)) / (1 - np.exp(decay))
    guard = HD * EPS * total * np.exp(-2 * (i % P)[:, None] * decay)
    c[:, C_GUARD:C_IDX] = guard.reshape(POS, P, H).transpose(1, 0, 2).reshape(P, POS * H)
    c[:, C_IDX:] = E - np.arange(E)
    sel = np.zeros((2 * E, E, P), np.float32)
    for e in range(E):
        sel[e, e] = sel[E + e, e] = 1
    at = np.arange(KD // 2, dtype=np.float32) * np.float32(1 / (KD // 2 - 1))
    angle = np.repeat((1 / 10000.0 ** at.astype(np.float64)).astype(np.float32), 2)
    phase = (i.astype(np.float32)[:, None] * angle[None, :]).astype(np.float64)
    sign = np.where(np.arange(KD) % 2 == 0, -1.0, 1.0)
    kscale = KD ** -0.5 * np.exp(-(i % P)[:, None] * decay)
    out = []
    for table in (np.cos(phase), np.sin(phase) * sign):
        q = np.tile(table, (1, H))
        k = (kscale[:, :, None] * table[:, None, :]).reshape(S, H * KD)
        both = np.concatenate([q, k], axis=1).reshape(POS, P, 2 * D)
        out.append(both.transpose(1, 0, 2).reshape(P, POS * 2 * D).astype(np.float32))
    return c, out[0], out[1], sel.reshape(2 * E, E * P)


def wait(eng, sem, value):
    if isinstance(value, int) and value <= 0:
        return
    eng.wait_ge(sem, value)


def within(n, end):
    return not isinstance(n, int) or 0 <= n < end


class Chain:

    def __init__(self, eng, sem, base):
        self.eng, self.sem, self.base, self.n = eng, sem, base, 0

    def step(self, ins):
        self.n += 1
        ins.then_inc(self.sem, 1)

    def wait(self):
        wait(self.eng, self.sem, self.base + self.n)

    def __call__(self, ins):
        self.step(ins)
        self.wait()


def newton_rsqrt(v, n, x, y, t, scale):
    if n == 0:
        return v.tensor_scalar(t.bitcast(I32), x.bitcast(I32), 1, None, ALU.logical_shift_right)
    if n == 1:
        return v.tensor_scalar(y.bitcast(I32), t.bitcast(I32), -1.0, RSQRT_MAGIC, ALU.mult, ALU.add)
    if n == NEWTON_LINKS - 1:
        return v.tensor_scalar(y, y, scale, None, ALU.mult)
    if n % 3 == 2:
        return v.scalar_tensor_tensor(out=t, in0=y, scalar=-0.5, in1=y, op0=ALU.mult, op1=ALU.mult)
    if n % 3 == 0:
        return v.tensor_tensor(t, t, x, ALU.mult)
    return v.scalar_tensor_tensor(out=y, in0=t, scalar=1.5, in1=y, op0=ALU.add, op1=ALU.mult)


def layernorm_stats(dve, chain, rows, stats):
    for c, x in enumerate(rows):
        chain.step(dve.bn_stats(out=stats[:, c, :], in_=x))


def layernorm_combine(dve, chain, stats, mv, v, t, sign=1.0):
    mean, half = mv[:, :, 0], mv[:, :, 1]
    chain.wait()
    chain.step(dve.scalar_tensor_tensor(out=v[:], in0=stats[:, :, 2], scalar=D * EPS, in1=stats[:, :, 5],
                                        op0=ALU.add, op1=ALU.add))
    chain.step(dve.tensor_tensor(mean, stats[:, :, 1], stats[:, :, 4], ALU.add))
    chain(dve.tensor_tensor(half, stats[:, :, 1], stats[:, :, 4], ALU.subtract))
    chain.step(dve.scalar_tensor_tensor(out=t[:], in0=half, scalar=0.25, in1=half, op0=ALU.mult, op1=ALU.mult))
    chain(dve.tensor_scalar(mean, mean, 0.5 * sign, None, ALU.mult))
    chain.step(dve.scalar_tensor_tensor(out=v[:], in0=v[:], scalar=1.0 / D, in1=t[:], op0=ALU.mult, op1=ALU.add))


def setup(nc, sb, sem, args, T):
    ld, done = sem("const_loaded"), sem("split_done")
    loads = [sem(f"weights_loaded{i}") for i in range(5)]
    sel_loaded = sem("sel_loaded")
    part, ones = sem("hi_part_done"), sem("ones_done")
    with nc.Block() as block:
        @block.sync
        def _(sp):
            sp.dma_start(T["consts"][:], args["consts"]).then_inc(ld, 16)
            sp.dma_start(T["wall"][:], args["wall"]).then_inc(loads[0], 16)
            sp.dma_start(T["rw"][:], args["rw"]).then_inc(loads[1], 16)
            sp.dma_start(T["wo"][:], args["wo"]).then_inc(loads[2], 16)
            sp.dma_start(T["cos"][:], args["cos"]).then_inc(loads[3], 16)
            sp.dma_start(T["sin"][:], args["sin"]).then_inc(loads[4], 16)
            sp.dma_start(T["sel_staging"][:], args["sel"]).then_inc(sel_loaded, 16)
            sp.wait_ge(ld, 16)
            for s in loads:
                sp.wait_ge(s, 16)

        @block.scalar
        def _(act):
            act.wait_ge(loads[0], 16)
            act.activation(T["wall_hi"][:], T["wall"][:], ACT.Copy).then_inc(part, 1)

        @block.gpsimd
        def _(pool):
            for n in range(PAIRS):
                pool.memset(T["v32"][n][:, :, :, HD:HA], 1.0).then_inc(ones, 1)
                pool.memset(T["v_hi"][n][:, :, :, HD:HA], 1.0).then_inc(ones, 1)
                pool.memset(T["v_lo"][n][:, :, :, HD:HA], 0.0).then_inc(ones, 1)
            pool.memset(T["minus_half"][:], -0.5).then_inc(ones, 1)
            pool.wait_ge(ones, 3 * PAIRS + 1)

        @block.vector
        def _(dve):
            for n in ("rw_hi", "rw_lo"):
                dve.memset(T[n][:].bitcast(F32), 0.0).then_inc(done, 1)
            dve.wait_ge(loads[1], 16)
            dve.wait_ge(done, 2)
            dve.tensor_copy(T["rw_hi"][:, 0:E], T["rw"][:]).then_inc(done, 1)
            dve.wait_ge(done, 3)
            dve.tensor_tensor(T["rw_lo"][:, 0:E], T["rw"][:], T["rw_hi"][:, 0:E].bitcast(F32),
                              ALU.subtract).then_inc(done, 1)
            dve.wait_ge(part, 1)
            dve.tensor_tensor(T["wall_lo"][:], T["wall"][:], T["wall_hi"][:].bitcast(F32),
                              ALU.subtract).then_inc(done, 1)
            dve.wait_ge(sel_loaded, 16)
            dve.tensor_copy(T["sel"][:], T["sel_staging"][:]).then_inc(done, 1)
            dve.wait_ge(done, 6)


def attention(nc, st, sb, ps, sem, args, T):
    con = T["consts"]
    ident = con[:, C_ID:C_ID + P]
    tri = con[:, C_TRI:C_TRI + P].rearrange("p (o i) -> p o i", o=1).broadcast_to([P, 4, P])
    par_mask = [con[:, C_EVEN:C_EVEN + 1], con[:, C_ODD:C_ODD + 1]]

    xT = [sb(f"xT{i}", [P, 2 * P], F32) for i in range(2)]
    xT_hi = [sb(f"xT_hi{i}", [P, 2 * P], F32R) for i in range(2)]
    xT_lo = [sb(f"xT_lo{i}", [P, 2 * P], F32R) for i in range(2)]
    x_tok = [sb(f"x_tok{i}", [P, 4, D], F32) for i in range(2)]
    rot_a, rot_b = sb("rot_a", [P, 4 * D], F32), sb("rot_b", [P, 4 * D], F32)
    qk_tok = [sb(f"qk_tok{i}", [P, 2, 2 * D], F32) for i in range(2)]
    v32, v_hi, v_lo = T["v32"], T["v_hi"], T["v_lo"]
    gate = [sb(f"gate{i}", [P, 4, V], F32) for i in range(2)]
    q32 = [sb(f"q32_{i}", [P, 2, P], F32) for i in range(PAIRS)]
    q_hi = [sb(f"q_hi{i}", [P, 2, 2, P], F32R) for i in range(2)]
    q_lo = [sb(f"q_lo{i}", [P, 2, 2, P], F32R) for i in range(2)]
    k_hi = [sb(f"k_hi{i}", [P, 2, P], F32R) for i in range(2)]
    k_lo = [sb(f"k_lo{i}", [P, 2, P], F32R) for i in range(2)]
    s32 = [sb(f"s32_{g}", [P, 4 * P], F32) for g in range(4)]
    s_hi = [[sb(f"s_hi{i}_{g}", [P, 4 * P], BF16) for g in range(4)] for i in range(2)]
    s_lo = [[sb(f"s_lo{i}_{g}", [P, 4 * P], BF16) for g in range(4)] for i in range(2)]
    state = [sb(f"state{i}", [P, H * HA], F32) for i in range(2)]
    kv_masked = [sb(f"kv_masked{i}", [P, H * HA], F32) for i in range(2)]
    o_sb = [sb(f"o_sb{i}", [P, 4, H, HA], F32) for i in range(2)]
    o_sq = [sb(f"o_sq{i}", [P, H, HD], F32) for i in range(2)]
    o_ms = [sb(f"o_ms{i}", [P, 4, H], F32) for i in range(2)]
    rms_v, rms_t = sb("rms_v", [P, 4 * H], F32), sb("rms_t", [P, 4 * H], F32)
    rms_r = sb("rms_r", [P, 4 * H], F32)
    gated = sb("gated", [P, 4, V], F32)
    gT = sb("gT", [P, 4, 2, P], F32)
    resid = sb("resid", [P, 4, D], F32)
    ln_st, ln_mv = sb("ln_st", [P, 4, 6], F32), sb("ln_mv", [P, 4, 2], F32)
    ln_v, ln_t, ln_r = (sb(f"ln_{c}", [P, 4], F32) for c in "vtr")
    ln_shift = sb("ln_shift", [P, 4], F32)
    lgT = sb("lgT", [P, GT], F32)

    ps_s = [ps(f"ps_s{g}", [P, 4 * P]) for g in range(4)]
    ps_o, ps_vg, ps_qk, ps_t = ps("ps_o", [P, 4 * P]), ps("ps_vg", [P, 4 * P]), ps("ps_qk", [P, 4 * P]), ps("ps_t", [P, 4 * P])

    xT_loaded = [sem(f"xT_loaded{i}") for i in range(2)]
    x_tok_loaded = [sem(f"x_tok_loaded{i}") for i in range(2)]
    xhi_done, xlo_done = sem("xhi_done"), sem("xlo_done")
    qk_proj, vg_proj = sem("qk_proj"), sem("vg_proj")
    rope_done, qktok_done, qkT_done = sem("rope_done"), sem("qktok_done"), sem("qkT_done")
    qkhi_done, qklo_done = sem("qkhi_done"), sem("qklo_done")
    v_done, vlo_done = sem("v_done"), sem("vlo_done")
    scores_done, s32_done = sem("scores_done"), sem("s32_done")
    shi_done, slo_done = sem("shi_done"), sem("slo_done")
    kv_done, kv_read, state_done = sem("kv_done"), sem("kv_read"), sem("state_done")
    o_done, osb_done, ms_done = sem("o_done"), sem("osb_done"), sem("ms_done")
    rms_chain, go_done, gated_done = sem("rms_chain"), sem("go_done"), sem("gated_done")
    gT_done, gT_read, wo_done = sem("gT_done"), sem("gT_read"), sem("wo_done")
    ln_chain, h1T_done = sem("ln_chain"), sem("h1T_done")
    h1hi_done, h1lo_done = sem("h1hi_done"), sem("h1lo_done")
    lgT_done, lgT_read, lg_done, lg_read = sem("lgT_done"), sem("lgT_read"), sem("lg_done"), sem("lg_read")
    ln_r_done, h1_done = sem("ln_r_done"), sem("h1_done")
    RMS_SUM = 3
    RMS_LINKS = RMS_SUM + NEWTON_LINKS
    LN_LINKS = 1 + LN_STATS + LN_COMBINE

    def steps(eng, body):
        for pp in range(-3, PAIRS):
            body(0, pp)
        for pp in range(PAIRS):
            body(1, pp)
        with eng.Fori(2, B - 1) as b:
            for pp in range(PAIRS):
                body(b, pp)
        for pp in range(PAIRS):
            body(B - 1, pp)
        for pp in range(PAIRS + 1):
            body(B, pp)

    def tail(b, pp):
        g = 2 * b + pp // 2
        if pp % 2 == 0:
            return g - 1, g - 2, g - 3
        return g - 1, g - 2

    def kv_before(b, pp):
        return (POS - 1) * b + min(2 * max(pp, 0), POS - 1)

    with nc.Block() as block:
        @block.sync
        def _(sp):
            def body(b, pp):
                n = PAIRS * b + pp
                if within(n + 3, NPAIR):
                    j = (pp + 1) % 2
                    wait(sp, xhi_done, n + 2)
                    wait(sp, xlo_done, n + 2)
                    sp.dma_start(xT[j][:], args["xT"][:, ds((n + 3) * 2 * P, 2 * P)]).then_inc(xT_loaded[j], 16)
                if within(n, NPAIR) and pp % 2 == 1:
                    g = 2 * b + pp // 2
                    wait(sp, ln_chain, LN_LINKS * (g - 2) + 1)
                    sp.dma_start(x_tok[pp // 2 % 2][:],
                                 args["x"][ds(g * GT, GT), :].rearrange("(c p) d -> p c d", p=P)
                                 ).then_inc(x_tok_loaded[pp // 2 % 2], 16)
            steps(sp, body)

        @block.tensor
        def _(pe):
            def three_pass(out, w_hi, w_lo, x_hi, x_lo, first=True, last=True):
                pe.matmul(out, w_hi, x_hi, start=first, stop=False)
                pe.matmul(out, w_hi, x_lo, start=False, stop=False)
                return pe.matmul(out, w_lo, x_hi, start=False, stop=last)

            def project_vg(n, i, c):
                x = slice(c * P, (c + 1) * P)
                three_pass(ps_vg[:], xT_hi[i][:, x], xT_lo[i][:, x], T["wall_hi"][:, 2 * D:],
                           T["wall_lo"][:, 2 * D:]).then_inc(vg_proj, 1)

            def tail_part(b, pp, part):
                if pp % 2 == 0:
                    g = tail(b, pp)[2]
                    if part == 0 and within(g, GROUPS):
                        pe.wait_ge(lgT_read, g + 1)
                        for c in range(4):
                            mm = pe.transpose(ps_t[:, c * P:(c + 1) * P], lgT[:, c * P:(c + 1) * P], ident)
                        mm.then_inc(lg_done, 1)
                    return
                g = tail(b, pp)[0]
                if not within(g, GROUPS):
                    return
                if part == 0:
                    pe.wait_ge(gated_done, g + 1)
                    wait(pe, h1hi_done, g)
                    wait(pe, h1lo_done, g)
                else:
                    pe.wait_ge(gT_read, 2 * g + 1)
                for k in range(4):
                    mm = pe.transpose(ps_t[:, k * P:(k + 1) * P],
                                      gated[:, 2 * part + k // 2, (k % 2) * P:(k % 2 + 1) * P], ident)
                mm.then_inc(gT_done, 1)

            def project_out(b, pp):
                g = tail(b, pp)[1]
                if within(g, GROUPS):
                    pe.wait_ge(gT_read, 2 * g + 2)
                    for c in range(4):
                        for k in range(2):
                            mm = pe.matmul(ps_t[:, c * P:(c + 1) * P], gT[:, c, k, :], T["wo"][:, k * D:(k + 1) * D],
                                           start=(k == 0), stop=(k == 1))
                    mm.then_inc(wo_done, 1)

            def body(b, pp):
                n = PAIRS * b + pp
                i, j = pp % 2, (pp + 1) % 2
                main, front = within(n, NPAIR), within(n + 1, NPAIR)
                ahead = within(n + 2, NPAIR)

                def update(c):
                    pos = 2 * pp + c
                    if pos < POS - 1:
                        wait(pe, kv_read, (POS - 1) * b + pos)
                        pe.matmul(ps_vg[:, 0:H * HA], qk_tok[i][:, c, D:2 * D],
                                  v32[pp % PAIRS][:, c, :, :].rearrange("p h a -> p (h a)"),
                                  start=True, stop=True).then_inc(kv_done, 1)

                def values(c):
                    pos, m = 2 * pp + c, 2 * n + c
                    pe.wait_ge(vlo_done, m + 1)
                    wait(pe, osb_done, 2 * m)
                    for h in range(H):
                        if c == 0 and h % 2 == 0:
                            pe.wait_ge(shi_done, 4 * n + h // 2 + 1)
                            pe.wait_ge(slo_done, 4 * n + h // 2 + 1)
                        cols = slice((2 * c + h % 2) * P, (2 * c + h % 2 + 1) * P)
                        o = ps_o[:, h * HA:(h + 1) * HA]
                        for k, (s, v) in enumerate(((s_hi, v_hi), (s_hi, v_lo), (s_lo, v_hi))):
                            mm = pe.matmul(o, s[i][h // 2][:, cols], v[pp % PAIRS][:, c, h, :], start=(h == 0 and k == 0),
                                           stop=(pos == 0), skip_group_check=True)
                    if pos:
                        if pos == 1:
                            pe.wait_ge(kv_read, (POS - 1) * b + 1)
                        else:
                            pe.wait_ge(state_done, (POS - 2) * b + pos - 1)
                        mm = pe.matmul(ps_o[:, 0:H * HA], q32[pp % PAIRS][:, c, :], state[pos % 2][:],
                                       start=False, stop=True, skip_group_check=True)
                    mm.then_inc(o_done, 1)

                def first_vg():
                    if ahead:
                        wait(pe, v_done, 6 * (n + 2))
                        wait(pe, kv_read, kv_before(b, pp + 1))
                        project_vg(n + 2, i, 0)

                def second_vg():
                    if ahead:
                        pe.wait_ge(v_done, 6 * (n + 2) + 3)
                        project_vg(n + 2, i, 1)

                def scores(g):
                    wait(pe, s32_done, 4 * n + g + 1)
                    rows = slice(32 * g, 32 * g + 32)
                    for c in range(2):
                        mm = three_pass(ps_s[g][:, c * 2 * P:(c + 1) * 2 * P], k_hi[j][rows, c, :],
                                        k_lo[j][rows, c, :], q_hi[j][rows, c, :, :], q_lo[j][rows, c, :, :])
                    mm.then_inc(scores_done, 1)

                if front and main:
                    pe.wait_ge(v_done, 6 * (n + 2))
                if main:
                    update(0)
                if front:
                    pe.wait_ge(qkhi_done, 4 * (n + 2))
                    pe.wait_ge(qklo_done, 3 * (n + 2))
                if ahead:
                    pe.wait_ge(xhi_done, n + 3)
                    pe.wait_ge(xlo_done, n + 3)
                    for c in range(2):
                        x = slice(c * P, (c + 1) * P)
                        mm = three_pass(ps_qk[:, c * 2 * D:(c + 1) * 2 * D], xT_hi[i][:, x], xT_lo[i][:, x],
                                        T["wall_hi"][:, 0:2 * D], T["wall_lo"][:, 0:2 * D])
                    mm.then_inc(qk_proj, 1)
                if main:
                    update(1)
                if pp % 2 == 0:
                    project_out(b, pp)
                if front:
                    scores(0)
                    scores(1)
                first_vg()
                if pp % 2 == 1:
                    g = tail(b, pp)[1]
                    if within(g, GROUPS):
                        pe.wait_ge(h1_done, 4 * (g + 1))
                        wait(pe, lg_read, g)
                        for c in range(4):
                            mm = pe.transpose(ps_t[:, c * P:(c + 1) * P], resid[:, c, :], ident)
                        mm.then_inc(h1T_done, 1)
                if front:
                    scores(2)
                    scores(3)
                if ahead:
                    pe.wait_ge(qktok_done, n + 3)
                    for k in range(4):
                        mm = pe.transpose(ps_qk[:, k * P:(k + 1) * P],
                                          qk_tok[i][:, k % 2, (k // 2) * D:(k // 2 + 1) * D], ident)
                    mm.then_inc(qkT_done, 1)
                if pp % 2 == 0:
                    _, summed, routed = tail(b, pp)
                    if within(routed, GROUPS):
                        pe.wait_ge(h1hi_done, routed + 1)
                        pe.wait_ge(h1lo_done, routed + 1)
                        if within(summed, GROUPS):
                            pe.wait_ge(ln_chain, LN_LINKS * summed + 1)
                        at = ds(routed * GT, GT)
                        three_pass(ps_t[:], T["rw_hi"][:], T["rw_lo"][:], T["h1T_hi"][:, at],
                                   T["h1T_lo"][:, at]).then_inc(lgT_done, 1)
                if main:
                    values(0)
                second_vg()
                if pp % 2 == 1:
                    tail_part(b, pp, 0)
                if main:
                    values(1)
                tail_part(b, pp, pp % 2)
            steps(pe, body)

        @block.scalar
        def _(act):
            def read_vg(b, pp, c):
                n, i, own = PAIRS * b + pp, pp % 2, pp % PAIRS
                act.wait_ge(vg_proj, 2 * n + c + 1)
                if c == 0:
                    wait(act, o_done, 2 * (n - 3))
                    wait(act, vlo_done, 2 * (n - 3))
                v = ps_vg[:, 0:V].rearrange("p (h d) -> p h d", d=HD)
                act.activation(v32[own][:, c, :, 0:HD], v, ACT.Copy).then_inc(v_done, 1)
                act.activation(v_hi[own][:, c, :, 0:HD], v, ACT.Copy).then_inc(v_done, 1)
                if c == 0:
                    wait(act, go_done, n - 3)
                act.activation(gate[pp // 2 % 2][:, 2 * i + c, :], ps_vg[:, V:2 * V], ACT.Silu
                               ).then_inc(v_done, 1)

            def tail_part(b, pp, part):
                g = tail(b, pp)[2 if pp % 2 == 0 else 0]
                if not within(g, GROUPS):
                    return
                if pp % 2 == 1:
                    if part == 0:
                        wait(act, wo_done, g)
                    act.wait_ge(gT_done, 2 * g + part + 1)
                    act.activation(gT[:, 2 * part:2 * part + 2, :, :],
                                   ps_t[:].rearrange("p (c k i) -> p c k i", c=2, k=2), ACT.Copy
                                   ).then_inc(gT_read, 1)
                else:
                    act.wait_ge(lg_done, g + 1)
                    act.activation(T["logits"][:, ds(g * 4 * E, 4 * E)].rearrange("p (c e) -> p c e", e=E),
                                   ps_t[:].rearrange("p (c e) -> p c e", e=P)[:, :, 0:E], ACT.Copy).then_inc(lg_read, 1)

            def body(b, pp):
                n = PAIRS * b + pp
                i, j = pp % 2, (pp + 1) % 2
                main, front = within(n, NPAIR), within(n + 1, NPAIR)
                q = ps_qk[:, 0:2 * P].rearrange("p (c i) -> p c i", c=2)
                k = ps_qk[:, 2 * P:].rearrange("p (c i) -> p c i", c=2)

                def upper_scores(g):
                    if front:
                        wait(act, o_done, 2 * n)
                        act.wait_ge(s32_done, 4 * (n + 1) + g + 1)
                        act.activation(s_hi[j][g][:], s32[g][:], ACT.Copy).then_inc(shi_done, 1)

                def upper_qk():
                    if within(n + 2, NPAIR):
                        act.wait_ge(qkT_done, n + 3)
                        for par in range(2):
                            act.activation(q_hi[i][:, :, par, :], q, ACT.Copy, scale=par_mask[par]
                                           ).then_inc(qkhi_done, 1)
                        act.activation(k_hi[i][:], k, ACT.Copy).then_inc(qkhi_done, 1)
                        act.activation(q32[(pp + 2) % PAIRS][:], q, ACT.Copy).then_inc(qkhi_done, 1)

                def read_o(c):
                    if not main:
                        return
                    m = 2 * n + c
                    act.wait_ge(o_done, m + 1)
                    o = ps_o[:, 0:H * HA].rearrange("p (h a) -> p h a", a=HA)
                    act.activation(o_sb[pp // 2 % 2][:, 2 * i + c, :, :], o, ACT.Copy).then_inc(osb_done, 1)
                    wait(act, ms_done, m - 1)
                    act.activation(o_sq[c][:], o[:, :, 0:HD], ACT.Square).then_inc(osb_done, 1)

                g = tail(b, pp)[2 if pp % 2 == 0 else 1]
                if pp % 2 == 1 and within(g, GROUPS):
                    act.wait_ge(ln_r_done, 2 * (g + 1))
                    for c in range(4):
                        act.activation(resid[:, c, :], resid[:, c, :], ACT.Identity, scale=ln_r[:, c:c + 1],
                                       bias=ln_shift[:, c:c + 1]).then_inc(h1_done, 1)
                if within(n + 3, NPAIR):
                    act.wait_ge(xT_loaded[j], 16 * (2 * b + (pp + 3) // 2 + 1))
                    wait(act, vg_proj, 2 * (n + 2))
                    wait(act, xlo_done, n + 2)
                    act.activation(xT_hi[j][:], xT[j][:], ACT.Copy).then_inc(xhi_done, 1)
                if within(n + 2, NPAIR):
                    read_vg(b, pp + 2, 0)
                upper_scores(0)
                if pp % 2 == 1 and within(g, GROUPS):
                    act.wait_ge(h1T_done, g + 1)
                    act.activation(T["h1T_hi"][:, ds(g * GT, GT)], ps_t[:], ACT.Copy).then_inc(h1hi_done, 1)
                upper_scores(1)
                upper_scores(2)
                upper_qk()
                if main and pp % 2 == 0:
                    wait(act, gated_done, 2 * b + pp // 2 - 1)
                read_o(0)
                upper_scores(3)
                if pp % 2 == 1:
                    tail_part(b, pp, 0)
                if pp % 2 == 0 and within(g, GROUPS):
                    act.wait_ge(lgT_done, g + 1)
                    wait(act, lg_done, g)
                    act.activation(lgT[:], ps_t[:], ACT.Copy).then_inc(lgT_read, 1)
                if within(n + 2, NPAIR):
                    read_vg(b, pp + 2, 1)
                read_o(1)
                tail_part(b, pp, pp % 2)
            steps(act, body)

        @block.gpsimd
        def _(pool):
            def v_lower(n, j, c):
                j = j % PAIRS
                pool.wait_ge(v_done, 6 * (n + 1) + 3 * c + 2)
                pool.tensor_tensor(v_lo[j][:, c, :, 0:HD], v32[j][:, c, :, 0:HD], v_hi[j][:, c, :, 0:HD],
                                   ALU.subtract).then_inc(vlo_done, 1)

            def body(b, pp):
                n = PAIRS * b + pp
                i, j = pp % 2, (pp + 1) % 2
                main, front = within(n, NPAIR), within(n + 1, NPAIR)
                def lower_scores(g):
                    if front:
                        wait(pool, o_done, 2 * n)
                        pool.wait_ge(shi_done, 4 * (n + 1) + g + 1)
                        pool.tensor_tensor(s_lo[j][g][:], s32[g][:], s_hi[j][g][:], ALU.subtract).then_inc(slo_done, 1)

                if front:
                    v_lower(n, pp + 1, 0)
                    v_lower(n, pp + 1, 1)
                if within(n - 1, NPAIR):
                    pool.wait_ge(osb_done, 4 * n)
                    pool.wait_ge(v_done, 6 * n)
                    o = o_sb[(pp - 1) // 2 % 2][:, 2 * j:2 * j + 2, :, 0:HD]
                    by_head = "p c (h d) -> p c h d"
                    pool.tensor_tensor(o, gate[(pp - 1) // 2 % 2][:, 2 * j:2 * j + 2, :].rearrange(by_head, d=HD), o,
                                       ALU.mult).then_inc(go_done, 1)
                if within(n + 2, NPAIR):
                    pool.wait_ge(rope_done, 2 * (n + 3))
                    wait(pool, kv_done, kv_before(b, pp + 1))
                    pool.tensor_tensor(qk_tok[i][:].rearrange("p c d -> p (c d)"), rot_a[:], rot_b[:], ALU.add
                                       ).then_inc(qktok_done, 1)
                lower_scores(0)
                lower_scores(1)
                if within(n + 3, NPAIR):
                    pool.wait_ge(xhi_done, n + 4)
                    pool.tensor_tensor(xT_lo[j][:], xT[j][:], xT_hi[j][:].bitcast(F32), ALU.subtract
                                       ).then_inc(xlo_done, 1)
                lower_scores(2)
                lower_scores(3)
                if pp % 2 == 0:
                    summed = tail(b, pp)[1]
                    if within(summed, GROUPS):
                        pool.wait_ge(ln_chain, LN_LINKS * (summed + 1))
                        wait(pool, h1_done, 4 * summed)
                        pool.tensor_tensor(ln_r[:], ln_v[:], T["minus_half"][:], ALU.pow).then_inc(ln_r_done, 1)
                        pool.wait_ge(ln_r_done, 2 * summed + 1)
                        pool.tensor_tensor(ln_shift[:], ln_mv[:, :, 0], ln_r[:], ALU.mult).then_inc(ln_r_done, 1)
            steps(pool, body)

        @block.vector
        def _(dve):
            def square_sum(b, pp, c):
                dve.wait_ge(osb_done, 2 * (2 * (PAIRS * b + pp) + c + 1))
                dve.tensor_reduce(o_ms[pp // 2 % 2][:, 2 * (pp % 2) + c, :], o_sq[c][:], AX_X, ALU.add
                                  ).then_inc(ms_done, 1)

            def body(b, pp):
                n = PAIRS * b + pp
                i, j = pp % 2, (pp + 1) % 2
                main, front = within(n, NPAIR), within(n + 1, NPAIR)
                even = pp % 2 == 0
                rooted, summed = (tail(b, pp)[0], tail(b, pp)[1]) if even else (-1, -1)
                gating, applied = (-1, -1) if even else tail(b, pp)
                rms = Chain(dve, rms_chain, RMS_LINKS * rooted)

                def rms_link():
                    if not within(rooted, GROUPS) or rms.n == RMS_LINKS:
                        return
                    v = rms_v[:].rearrange("p (c h) -> p c h", h=H)
                    half = (pp // 2 - 1) % 2
                    rms.wait()
                    if rms.n == 0:
                        dve.wait_ge(osb_done, 8 * (rooted + 1))
                        total = o_sb[half][:, :, :, HD]
                        rms.step(dve.scalar_tensor_tensor(out=v, in0=total, scalar=HD * EPS, in1=total,
                                                          op0=ALU.mult, op1=ALU.mult))
                    elif rms.n == 1:
                        guard = con[:, C_GUARD + half * 4 * H:C_GUARD + (half + 1) * 4 * H]
                        rms.step(dve.tensor_tensor(rms_v[:], rms_v[:], guard, ALU.max))
                    elif rms.n == 2:
                        dve.wait_ge(ms_done, 4 * (rooted + 1))
                        rms.step(dve.tensor_tensor(v, v, o_ms[half][:], ALU.add))
                    else:
                        if rms.n == RMS_SUM + 1:
                            wait(dve, gated_done, rooted)
                        rms.step(newton_rsqrt(dve, rms.n - RMS_SUM, rms_v[:], rms_r[:], rms_t[:], float(HD) ** 0.5))

                rows = [resid[:, c, :] for c in range(4)]
                def product_read(c):
                    pos, m = 2 * pp + c, 2 * n + c
                    if pos < POS - 1:
                        dve.wait_ge(kv_done, (POS - 1) * b + pos + 1)
                        if pos == 0:
                            wait(dve, o_done, m)
                        wait(dve, state_done, (POS - 2) * b + max(pos - 2, 0))
                        out = state[1] if pos == 0 else kv_masked[c]
                        dve.tensor_tensor(out[:], ps_vg[:, 0:H * HA], con[:, C_DECAY:C_GAMMA], ALU.mult
                                          ).then_inc(kv_read, 1)

                def state_update(c):
                    pos, m = 2 * pp + c, 2 * n + c
                    rms_link()
                    if 0 < pos < POS - 1:
                        dve.wait_ge(kv_read, (POS - 1) * b + pos + 1)
                        wait(dve, o_done, m)
                        dve.scalar_tensor_tensor(out=state[(pos + 1) % 2][:], in0=state[pos % 2][:],
                                                 scalar=con[:, C_GAMMA:C_GAMMA + 1], in1=kv_masked[c][:],
                                                 op0=ALU.mult, op1=ALU.add).then_inc(state_done, 1)

                def causal(g):
                    if front:
                        rms_link()
                        if g == 0:
                            rms_link()
                        dve.wait_ge(scores_done, 4 * (n + 1) + g + 1)
                        wait(dve, slo_done, 4 * n + g + 1)
                        dve.tensor_tensor(s32[g][:].rearrange("p (r i) -> p r i", i=P),
                                          ps_s[g][:].rearrange("p (r i) -> p r i", i=P), tri, ALU.mult
                                          ).then_inc(s32_done, 1)

                if main:
                    product_read(0)
                if within(n + 2, NPAIR):
                    dve.wait_ge(qk_proj, n + 3)
                    wait(dve, qktok_done, n + 2)
                    at = slice((pp + 2) % PAIRS * 4 * D, ((pp + 2) % PAIRS + 1) * 4 * D)
                    two = "p (d t) -> p d t"
                    dve.tensor_tensor(rot_a[:], ps_qk[:], T["cos"][:, at], ALU.mult).then_inc(rope_done, 1)
                if main:
                    product_read(1)
                if within(n + 2, NPAIR):
                    rms_link()
                    dve.tensor_tensor(rot_b[:].rearrange(two, t=2), ps_qk[:].rearrange(two, t=2)[:, :, ::-1],
                                      T["sin"][:, at].rearrange(two, t=2), ALU.mult).then_inc(rope_done, 1)
                if within(n - 1, NPAIR):
                    square_sum(b, pp - 1, 1)
                if main:
                    state_update(0)
                causal(0)
                causal(1)
                if within(summed, GROUPS):
                    ln = Chain(dve, ln_chain, LN_LINKS * summed)
                    ln.wait()
                    wait(dve, h1T_done, summed)
                    dve.wait_ge(wo_done, summed + 1)
                    dve.wait_ge(x_tok_loaded[pp // 2 % 2], 16 * (b + pp // 2 // 2))
                    ln.step(dve.tensor_tensor(resid[:].rearrange("p c d -> p (c d)"), ps_t[:],
                                              x_tok[pp // 2 % 2][:].rearrange("p c d -> p (c d)"), ALU.add))
                causal(2)
                causal(3)
                if within(applied, GROUPS):
                    dve.wait_ge(h1hi_done, applied + 1)
                    at = ds(applied * GT, GT)
                    dve.tensor_tensor(T["h1T_lo"][:, at], ps_t[:], T["h1T_hi"][:, at].bitcast(F32), ALU.subtract
                                      ).then_inc(h1lo_done, 1)
                if within(gating, GROUPS):
                    dve.wait_ge(rms_chain, RMS_LINKS * (gating + 1))
                    dve.wait_ge(go_done, 2 * (gating + 1))
                    wait(dve, gT_done, 2 * gating)
                    r = rms_r[:].rearrange("p (h o) -> p h o", o=1).broadcast_to([P, 4 * H, HD])
                    dve.tensor_tensor(gated[:].rearrange("p c (h d) -> p (c h) d", d=HD),
                                      o_sb[(pp // 2 - 1) % 2][:, :, :, 0:HD].rearrange("p c h d -> p (c h) d"), r,
                                      ALU.mult).then_inc(gated_done, 1)
                rms_link()
                if within(n + 2, NPAIR):
                    dve.wait_ge(qkhi_done, 4 * (n + 3))
                    q = ps_qk[:, 0:2 * P].rearrange("p (c i) -> p c i", c=2)
                    k = ps_qk[:, 2 * P:].rearrange("p (c i) -> p c i", c=2)
                    for par in range(2):
                        dve.scalar_tensor_tensor(out=q_lo[i][:, :, par, :], in0=q, scalar=par_mask[par],
                                                 in1=q_hi[i][:, :, par, :].bitcast(F32), op0=ALU.mult,
                                                 op1=ALU.subtract).then_inc(qklo_done, 1)
                        rms_link()
                    dve.tensor_tensor(k_lo[i][:], k, k_hi[i][:].bitcast(F32), ALU.subtract).then_inc(qklo_done, 1)
                rms_link()
                if within(summed, GROUPS):
                    ln = Chain(dve, ln_chain, LN_LINKS * summed + 1)
                    ln.wait()
                    layernorm_stats(dve, ln, rows, ln_st)
                rms_link()
                if within(summed, GROUPS):
                    wait(dve, ln_r_done, 2 * summed)
                    layernorm_combine(dve, Chain(dve, ln_chain, LN_LINKS * summed + 1 + LN_STATS), ln_st, ln_mv,
                                      ln_v, ln_t, sign=-1.0)
                if main:
                    state_update(1)
                    square_sum(b, pp, 0)
                while within(rooted, GROUPS) and rms.n < RMS_LINKS:
                    rms_link()
            steps(dve, body)


def routing(nc, sb, ps, sem, args, T):
    W = NCH * E
    lg = T["logits"]
    con = T["consts"]
    by = "p (n e) -> p n e"
    hot1, hot2, tmp, left = (sb(n, [P, W], F32) for n in ("hot1", "hot2", "tmp", "left"))
    top1, top2, at, gap, ratio, den, w1, w2 = (sb(n, [P, NCH], F32) for n in (
        "top1", "top2", "at", "gap", "ratio", "den", "w1", "w2"))
    wts = sb("wts", [P, W], F32)
    parts = sb("parts", [P, NCH, 2 * E], F32R)
    banks = [ps(f"ps_w{n}", [2 * E, GT]) for n in range(8)]
    chain, exp_done, parts_done = sem("routing_chain"), sem("exp_done"), sem("parts_done")
    tr_done, read_even, read_odd = sem("weights_transposed"), sem("read_even"), sem("read_odd")
    ehi, elo = sem("experts_hi_done"), sem("experts_lo_done")
    loaded = [sem(f"experts_loaded{n}") for n in range(3)]
    experts = sb("experts", [P, E * 3 * F], F32)
    idx = con[:, C_IDX:C_IDX + E].rearrange("p (o e) -> p o e", o=1).broadcast_to([P, NCH, E])

    def each(col):
        return col[:].rearrange("p (n o) -> p n o", o=1).broadcast_to([P, NCH, E])

    def table(t):
        return t[:].rearrange(by, e=E)

    THIRD = E * F
    with nc.Block() as block:
        @block.sync
        def _(sp):
            for n in range(3):
                source = args["gu"][:, n * THIRD:(n + 1) * THIRD] if n < 2 else args["dp"]
                sp.dma_start(experts[:, n * THIRD:(n + 1) * THIRD], source).then_inc(loaded[n], 16)

        @block.vector
        def _(dve):
            link = Chain(dve, chain, 0)
            scores = lg
            for top, hot in ((top1, hot1), (top2, hot2)):
                link(dve.tensor_reduce(top[:], table(scores), AX_X, ALU.max))
                link(dve.tensor_tensor(table(tmp), table(scores), each(top), ALU.is_equal))
                link(dve.tensor_tensor(table(tmp), table(tmp), idx, ALU.mult))
                link(dve.tensor_reduce(at[:], table(tmp), AX_X, ALU.max))
                link(dve.tensor_tensor(table(hot), idx, each(at), ALU.is_equal))
                if top is top1:
                    link(dve.scalar_tensor_tensor(out=left[:], in0=hot[:], scalar=-3.0e38, in1=lg[:],
                                                  op0=ALU.mult, op1=ALU.add))
                    scores = left
            link(dve.tensor_tensor(gap[:], top2[:], top1[:], ALU.subtract))
            dve.wait_ge(exp_done, 1)
            link(dve.tensor_scalar(den[:], ratio[:], 1.0, None, ALU.add))
            link(dve.reciprocal(w1[:], den[:]))
            link(dve.tensor_tensor(w2[:], ratio[:], w1[:], ALU.mult))
            link(dve.tensor_tensor(table(hot1), table(hot1), each(w1), ALU.mult))
            link(dve.tensor_tensor(table(hot2), table(hot2), each(w2), ALU.mult))
            link(dve.tensor_tensor(wts[:], hot1[:], hot2[:], ALU.add))
            link(dve.tensor_copy(parts[:, :, 0:E], table(wts)))
            dve.tensor_tensor(parts[:, :, E:2 * E], table(wts), parts[:, :, 0:E].bitcast(F32), ALU.subtract
                              ).then_inc(parts_done, 1)
            for g in range(1, GROUPS, 2):
                dve.wait_ge(tr_done, g + 1)
                dve.tensor_copy(T["wT"][:, g * GT:(g + 1) * GT], banks[g % 8][:]).then_inc(read_odd, 1)
            dve.wait_ge(read_odd, GROUPS // 2)

        @block.scalar
        def _(act):
            for n in range(3):
                part = slice(n * THIRD, (n + 1) * THIRD)
                act.wait_ge(loaded[n], 16)
                act.activation(T["experts_hi"][:, part], experts[:, part], ACT.Copy).then_inc(ehi, 1)
            act.wait_ge(chain, 12)
            act.activation(ratio[:], gap[:], ACT.Exp).then_inc(exp_done, 1)
            for g in range(0, GROUPS, 2):
                act.wait_ge(tr_done, g + 1)
                act.activation(T["wT"][:, g * GT:(g + 1) * GT], banks[g % 8][:], ACT.Copy).then_inc(read_even, 1)
            act.wait_ge(read_even, GROUPS // 2)

        @block.gpsimd
        def _(pool):
            for n in range(3):
                part = slice(n * THIRD, (n + 1) * THIRD)
                pool.wait_ge(ehi, n + 1)
                pool.tensor_tensor(T["experts_lo"][:, part], experts[:, part],
                                   T["experts_hi"][:, part].bitcast(F32), ALU.subtract).then_inc(elo, 1)
            pool.wait_ge(elo, 3)

        @block.tensor
        def _(pe):
            pe.wait_ge(parts_done, 1)
            for g in range(GROUPS):
                wait(pe, read_odd if g % 2 else read_even, (g - 8) // 2 + 1)
                for c in range(4):
                    mm = pe.transpose(banks[g % 8][:, c * P:(c + 1) * P], parts[:, 4 * g + c, :].bitcast(F32),
                                      con[:, C_ID:C_ID + P])
                mm.then_inc(tr_done, 1)


def experts(nc, sb, ps, sem, args, T):
    con = T["consts"]
    ident = con[:, C_ID:C_ID + P]
    act_s = [sb(f"act_s{i}", [P, GT], F32) for i in range(2)]
    w_sb = [sb(f"w_sb{i}", [P, GT], F32) for i in range(2)]
    uw = sb("uw", [P, GT], F32)
    a32 = [sb(f"a32_{i}", [P, GT], F32) for i in range(2)]
    a_hi = [sb(f"a_hi{i}", [P, GT], F32R) for i in range(2)]
    a_lo = [sb(f"a_lo{i}", [P, GT], F32R) for i in range(2)]
    h1T, z = sb("h1T", [P, GT], F32), sb("z", [P, GT], F32)
    z_tok = sb("z_tok", [P, GT], F32)
    ln_st, ln_mv = sb("ln2_st", [P, 4, 6], F32), sb("ln2_mv", [P, 4, 2], F32)
    ln_v, ln_t, ln_r = (sb(f"ln2_{c}", [P, 4], F32) for c in "vtr")
    y = [sb(f"y{i}", [P, 4, D], F32) for i in range(2)]
    ps_gate = [ps(f"ps_gate{i}", [P, GT]) for i in range(2)]
    ps_up = [ps(f"ps_up{i}", [P, GT]) for i in range(2)]
    ps_w = [ps(f"ps_wt{i}", [P, GT]) for i in range(2)]
    ps_acc = [ps(f"ps_acc{i}", [P, GT]) for i in range(2)]

    gate_mm, w_mm, up_mm = sem("gate_mm"), sem("w_mm"), sem("up_mm")
    silu_done, wsb_done, uw_done, a_done = sem("silu_done"), sem("wsb_done"), sem("uw_done"), sem("a_done")
    ahi_done, alo_done, down_mm = sem("ahi_done"), sem("alo_done"), sem("down_mm")
    h1_joined, z_done, zT_done, ztok_done = sem("h1_joined"), sem("z_done"), sem("zT_done"), sem("ztok_done")
    ln_chain, ln_r_done, y_done = sem("ln2_chain"), sem("ln2_r_done"), sem("y_done")
    stored = [sem(f"stored{i}") for i in range(2)]
    LN_LINKS = LN_STATS + LN_COMBINE
    ROUND = 2 * E
    TURNS = GROUPS // 2
    STEPS = GROUPS * E

    def steps(eng, body, ahead):
        for k in range(-ahead, ROUND):
            body(0, k)
        with eng.Fori(1, TURNS - 1) as t:
            for k in range(ROUND):
                body(t, k)
        for k in range(ROUND):
            body(TURNS - 1, k)
        for k in range(E):
            body(TURNS, k)

    with nc.Block() as block:
        @block.tensor
        def _(pe):
            def three_pass(out, w_hi, w_lo, x_hi, x_lo, first=True, last=True):
                pe.matmul(out, w_hi, x_hi, start=first, stop=False)
                pe.matmul(out, w_lo, x_hi, start=False, stop=False)
                return pe.matmul(out, w_hi, x_lo, start=False, stop=last)

            def body(t, k):
                n = ROUND * t + k
                if within(n + 2, STEPS):
                    e, i = (k + 2) % E, k % 2
                    at = ds((2 * t + (k + 2) // E) * GT, GT)
                    hi, lo = T["experts_hi"], T["experts_lo"]
                    xh, xl = T["h1T_hi"][:, at], T["h1T_lo"][:, at]
                    g = slice(e * 2 * F, e * 2 * F + F)
                    u = slice(e * 2 * F + F, (e + 1) * 2 * F)
                    wait(pe, silu_done, n + 1)
                    wait(pe, wsb_done, n + 1)
                    three_pass(ps_gate[i][:], hi[:, g], lo[:, g], xh, xl).then_inc(gate_mm, 1)
                    pe.matmul(ps_w[i][:], T["sel"][:, e * P:(e + 1) * P], T["wT"][:, at], start=True, stop=True
                              ).then_inc(w_mm, 1)
                    wait(pe, uw_done, n + 1)
                    three_pass(ps_up[i][:], hi[:, u], lo[:, u], xh, xl).then_inc(up_mm, 1)
                if within(n - 1, STEPS):
                    e, i = (k - 1) % E, (k - 1) % 2
                    w = slice(E * 2 * F + e * D, E * 2 * F + (e + 1) * D)
                    pe.wait_ge(alo_done, n)
                    pe.matmul(ps_acc[(k - 1) // E % 2][:], T["experts_hi"][:, w], a_lo[i][:], start=False,
                              stop=(e == E - 1)).then_inc(down_mm, 1)
                if within(n, STEPS):
                    e, i = k % E, k % 2
                    w = slice(E * 2 * F + e * D, E * 2 * F + (e + 1) * D)
                    acc = ps_acc[k // E % 2][:]
                    pe.wait_ge(ahi_done, n + 1)
                    if e == 0:
                        wait(pe, ztok_done, 2 * t + k // E - 1)
                    hi, lo = T["experts_hi"], T["experts_lo"]
                    pe.matmul(acc, hi[:, w], a_hi[i][:], start=(e == 0), stop=False)
                    pe.matmul(acc, lo[:, w], a_hi[i][:], start=False, stop=False)
                done = 2 * t + k // E - 1
                if k % E == 2 and within(done, GROUPS):
                    pe.wait_ge(z_done, done + 1)
                    bank = ps_acc[(k // E - 1) % 2]
                    for c in range(4):
                        mm = pe.transpose(bank[:, c * P:(c + 1) * P], z[:, c * P:(c + 1) * P], ident)
                    mm.then_inc(zT_done, 1)
            steps(pe, body, 2)

        @block.scalar
        def _(act):
            def body(t, k):
                n = ROUND * t + k
                if within(n + 1, STEPS):
                    i = (k + 1) % 2
                    act.wait_ge(gate_mm, n + 2)
                    wait(act, a_done, n)
                    act.activation(act_s[i][:], ps_gate[i][:], ACT.Silu).then_inc(silu_done, 1)
                    act.wait_ge(w_mm, n + 2)
                    wait(act, uw_done, n)
                    act.activation(w_sb[i][:], ps_w[i][:], ACT.Copy).then_inc(wsb_done, 1)
                if within(n, STEPS):
                    i = k % 2
                    act.wait_ge(a_done, n + 1)
                    wait(act, down_mm, n - 1)
                    act.activation(a_hi[i][:], a32[i][:], ACT.Copy).then_inc(ahi_done, 1)
                done = 2 * t + k // E - 1
                if k % E == 3 and within(done, GROUPS):
                    act.wait_ge(zT_done, done + 1)
                    wait(act, y_done, 4 * done)
                    act.activation(z_tok[:], ps_acc[(k // E - 1) % 2][:], ACT.Copy).then_inc(ztok_done, 1)
            steps(act, body, 1)

        @block.gpsimd
        def _(pool):
            def body(t, k):
                n = ROUND * t + k
                if within(n, STEPS):
                    i = k % 2
                    pool.wait_ge(ahi_done, n + 1)
                    wait(pool, down_mm, n - 1)
                    pool.tensor_tensor(a_lo[i][:], a32[i][:], a_hi[i][:].bitcast(F32), ALU.subtract
                                       ).then_inc(alo_done, 1)
                group = 2 * t + k // E
                done = group - 1
                if k % E == 6 and within(done, GROUPS):
                    pool.wait_ge(ln_chain, LN_LINKS * (done + 1))
                    wait(pool, y_done, 4 * done)
                    pool.tensor_tensor(ln_r[:], ln_v[:], T["minus_half"][:], ALU.pow).then_inc(ln_r_done, 1)
                if k % E == 4 and within(group, GROUPS):
                    at = ds(group * GT, GT)
                    wait(pool, z_done, group)
                    pool.tensor_tensor(h1T[:], T["h1T_hi"][:, at].bitcast(F32), T["h1T_lo"][:, at].bitcast(F32),
                                       ALU.add).then_inc(h1_joined, 1)
            steps(pool, body, 0)

        @block.vector
        def _(dve):
            def body(t, k):
                n = ROUND * t + k
                if within(n, STEPS):
                    i = k % 2
                    dve.wait_ge(wsb_done, n + 1)
                    dve.wait_ge(up_mm, n + 1)
                    wait(dve, a_done, n)
                    dve.tensor_tensor(uw[:], w_sb[i][:], ps_up[i][:], ALU.mult).then_inc(uw_done, 1)
                    dve.wait_ge(uw_done, n + 1)
                    dve.wait_ge(silu_done, n + 1)
                    wait(dve, alo_done, n - 1)
                    dve.tensor_tensor(a32[i][:], act_s[i][:], uw[:], ALU.mult).then_inc(a_done, 1)
                done, i = 2 * t + k // E - 1, (k // E - 1) % 2
                if k % E == 1 and within(done, GROUPS):
                    dve.wait_ge(down_mm, E * (done + 1))
                    dve.wait_ge(h1_joined, done + 1)
                    wait(dve, zT_done, done)
                    dve.tensor_tensor(z[:], ps_acc[i][:], h1T[:], ALU.add).then_inc(z_done, 1)
                if k % E in (4, 5) and within(done, GROUPS):
                    dve.wait_ge(ztok_done, done + 1)
                    first = 2 * (k % E - 4)
                    layernorm_stats(dve, Chain(dve, ln_chain, LN_LINKS * done + first),
                                    [z_tok[:, c * P:(c + 1) * P] for c in range(first, first + 2)],
                                    ln_st[:, first:first + 2, :])
                if k % E == 6 and within(done, GROUPS):
                    wait(dve, y_done, 4 * done)
                    layernorm_combine(dve, Chain(dve, ln_chain, LN_LINKS * done + LN_STATS), ln_st, ln_mv,
                                      ln_v, ln_t)
                if k % E == 7 and within(done, GROUPS):
                    dve.wait_ge(ln_chain, LN_LINKS * (done + 1))
                    dve.wait_ge(ln_r_done, done + 1)
                    wait(dve, stored[i], 16 * (t + (k // E - 1) // 2))
                    for c in range(4):
                        dve.tensor_scalar(y[i][:, c, :], z_tok[:, c * P:(c + 1) * P], ln_mv[:, c, 0:1],
                                          ln_r[:, c:c + 1], ALU.subtract, ALU.mult).then_inc(y_done, 1)
            steps(dve, body, 0)

        @block.sync
        def _(sp):
            def store(g, i):
                sp.wait_ge(y_done, 4 * (g + 1))
                sp.dma_start(args["out"][ds(g * GT, GT), :].rearrange("(c p) d -> p c d", p=P), y[i][:]
                             ).then_inc(stored[i], 16)
            with sp.Fori(0, TURNS) as t:
                for i in range(2):
                    store(2 * t + i, i)
            for i in range(2):
                sp.wait_ge(stored[i], 16 * TURNS)


def build(nc, args):
    T = {}
    with ExitStack() as keep:
        def pool_of(stack):
            def sb(name, shape, dt):
                return stack.enter_context(nc.sbuf_tensor(name, shape, dt))

            def ps(name, shape):
                return stack.enter_context(nc.psum_tensor(name, shape, F32))
            return sb, ps

        def sem(name):
            return keep.enter_context(nc.semaphore(name))

        sb, _ = pool_of(keep)
        T["consts"] = sb("consts", [P, C_END], F32)
        T["sel"] = sb("sel", [2 * E, E * P], F32R)
        T["h1T_hi"] = sb("h1T_hi", [P, B * S], F32R)
        T["h1T_lo"] = sb("h1T_lo", [P, B * S], F32R)
        T["minus_half"] = sb("minus_half", [P, 4], F32)
        T["logits"] = sb("logits", [P, NCH * E], F32)
        with ExitStack() as own:
            sb, ps = pool_of(own)
            for n, w in (("wo", 2 * D), ("cos", POS * 2 * D), ("sin", POS * 2 * D)):
                T[n] = sb(n, [P, w], F32)
            T["wall_hi"], T["wall_lo"] = (sb(n, [P, 2 * D + 2 * V], F32R) for n in ("wall_hi", "wall_lo"))
            T["rw_hi"], T["rw_lo"] = (sb(n, [P, P], F32R) for n in ("rw_hi", "rw_lo"))
            for n, dt in (("v32", F32), ("v_hi", BF16), ("v_lo", BF16)):
                T[n] = [sb(f"{n}_{i}", [P, 2, H, HA], dt) for i in range(PAIRS)]
            with ExitStack() as staging:
                T["wall"] = pool_of(staging)[0]("wall", [P, 2 * D + 2 * V], F32)
                T["rw"] = pool_of(staging)[0]("rw", [P, E], F32)
                T["sel_staging"] = pool_of(staging)[0]("sel_staging", [2 * E, E * P], F32)
                setup(nc, sb, sem, args, T)
            attention(nc, own, sb, ps, sem, args, T)
        T["wT"] = pool_of(keep)[0]("wT", [2 * E, B * S], F32R)
        T["experts_hi"] = pool_of(keep)[0]("experts_hi", [P, E * 3 * F], F32R)
        T["experts_lo"] = pool_of(keep)[0]("experts_lo", [P, E * 3 * F], F32R)
        with ExitStack() as own:
            routing(nc, *pool_of(own), sem, args, T)
        with ExitStack() as own:
            experts(nc, *pool_of(own), sem, args, T)


def kernel(**inputs):
    import concourse.bacc as bacc
    from concourse.bass_utils import run_bass_kernel_spmd

    consts, cos, sin, sel = shape_constants()
    a = {k: np.asarray(v) for k, v in inputs.items()}
    x = a["L0_attn_x"].reshape(B * S, D)
    arrays = {
        "x": np.ascontiguousarray(x),
        "xT": np.ascontiguousarray(x.T),
        "wall": np.ascontiguousarray(np.concatenate([a["L0_attn_" + n] for n in ("wq", "wk", "wv", "wg")], axis=1)),
        "wo": np.ascontiguousarray(a["L0_attn_wo"].reshape(2, P, D).transpose(1, 0, 2).reshape(P, 2 * D)),
        "rw": np.ascontiguousarray(a["L0_ffn_router_weight"].T),
        "gu": np.ascontiguousarray(a["L0_ffn_gate_up_proj"].transpose(2, 0, 1).reshape(D, E * 2 * F)),
        "dp": np.ascontiguousarray(a["L0_ffn_down_proj"].transpose(2, 0, 1).reshape(F, E * D)),
        "consts": consts, "cos": cos, "sin": sin, "sel": sel,
    }
    nc = bacc.Bacc("TRN2", target_bir_lowering=False, num_devices=1)
    args = {n: nc.dram_tensor(f"in_{n}", v.shape, mybir.dt.from_np(v.dtype), kind="ExternalInput").ap()
            for n, v in arrays.items()}
    args["out"] = nc.dram_tensor("out_y", (B * S, D), F32, kind="ExternalOutput").ap()
    build(nc, args)
    r = run_bass_kernel_spmd(nc, [{f"in_{n}": v for n, v in arrays.items()}], core_ids=[0])
    return r.results[0]["out_y"].reshape(B, S, D)
```
